# Optimizing a Trainium2 kernel written in Bass

```python
import numpy as np
import jax
import jax.numpy as jnp

def _softmax(x, axis=-1):
    return jax.nn.softmax(x, axis=axis)

def _gelu(x):
    return jax.nn.gelu(x, approximate=True)

def _silu(x):
    return jax.nn.silu(x)

def _sigmoid(x):
    return jax.nn.sigmoid(x)

def _layernorm(x, axis=-1, eps=1e-05):
    m = jnp.mean(x, axis=axis, keepdims=True)
    v = jnp.var(x, axis=axis, keepdims=True)
    return (x - m) / jnp.sqrt(v + eps)

def _scatter_add(tgt, idx, src, axis=0):
    return tgt.at[idx].add(src)

def _segment_sum(src, seg, n):
    return jax.ops.segment_sum(src, seg, n)
kernel_name = 'mk_adj_preln_d2_adj_r2_28f679'

def setup_inputs(seed: int=0):
    np.random.seed(seed)
    _w = jnp.asarray

    def _rec_inputs():
        import jax
        import jax.numpy as jnp
        _gk = jax.random.key(seed)
        x = 7.22e-05 + 1 * jax.random.normal(jax.random.fold_in(_gk, 1), (3327, 512), jnp.float32)
        _a = jax.random.bernoulli(jax.random.fold_in(_gk, 2), 0.00961827, (3327, 3327))
        _a = jnp.logical_or(_a, jnp.eye(3327, dtype=bool))
        _af = _a.astype(jnp.float32)
        _af = _af * jax.random.uniform(jax.random.fold_in(_gk, 3), (3327, 3327), jnp.float32, 0.05, 1)
        adj = _af
        return (x, adj)
    x, adj = _rec_inputs()

    def _L0_gnn_setup():
        import jax, jax.numpy as jnp
        import numpy as np
        N = 4096
        IN_FEATURES = 512
        OUT_FEATURES = 512
        key = jax.random.key(seed)
        k_x, k_adj, k_w, k_b = jax.random.split(key, 4)
        x = jax.random.normal(k_x, (N, IN_FEATURES), dtype=jnp.float32)
        adj = jax.random.uniform(k_adj, (N, N), dtype=jnp.float32)
        stdv = 1.0 / np.sqrt(OUT_FEATURES)
        weight = jax.random.uniform(k_w, (IN_FEATURES, OUT_FEATURES), dtype=jnp.float32, minval=-stdv, maxval=stdv)
        bias = jax.random.uniform(k_b, (OUT_FEATURES,), dtype=jnp.float32, minval=-stdv, maxval=stdv)
        return {'x': x, 'adj': adj, 'weight': weight, 'bias': bias}
    _L0_gnn_all = _L0_gnn_setup()
    _L0_gnn_in = {k: v for k, v in _L0_gnn_all.items() if k in ('weight', 'bias')}
    del _L0_gnn_all

    def _L1_gnn_setup():
        import jax, jax.numpy as jnp
        import numpy as np
        N, H, E, HEADS = (1500, 512, 10000, 8)
        DK = H // HEADS
        key = jax.random.key(seed)
        k1, k2, k3, k4 = jax.random.split(key, 4)
        inst_feature = jax.random.normal(k1, (N, H), dtype=jnp.float32)
        rel_pair_index = jax.random.randint(k2, (E, 2), 0, N, dtype=jnp.int64)
        agg = jnp.zeros((N, N), dtype=jnp.float32)
        agg = agg.at[rel_pair_index[:, 0], rel_pair_index[:, 1]].set(1.0)
        agg = agg.at[jnp.arange(N), jnp.arange(N)].set(1.0)
        std = float(np.sqrt(2.0 / (H + DK)))
        Wq = jax.random.normal(k3, (H, H), dtype=jnp.float32) * std
        Wk = jax.random.normal(k4, (H, H), dtype=jnp.float32) * std
        bq = jnp.zeros((H,), dtype=jnp.float32)
        bk = jnp.zeros((H,), dtype=jnp.float32)
        return {'inst_feature': inst_feature, 'aggregator_matrix': agg, 'rel_pair_index': rel_pair_index, 'Wq': Wq, 'bq': bq, 'Wk': Wk, 'bk': bk}
    _L1_gnn_all = _L1_gnn_setup()
    _L1_gnn_in = {k: v for k, v in _L1_gnn_all.items() if k in ('rel_pair_index', 'Wq', 'bq', 'Wk', 'bk')}
    del _L1_gnn_all
    return {'x': x, 'adj': adj, 'L0_gnn_weight': _L0_gnn_in['weight'], 'L0_gnn_bias': _L0_gnn_in['bias'], 'L1_gnn_rel_pair_index': _L1_gnn_in['rel_pair_index'], 'L1_gnn_Wq': _L1_gnn_in['Wq'], 'L1_gnn_bq': _L1_gnn_in['bq'], 'L1_gnn_Wk': _L1_gnn_in['Wk'], 'L1_gnn_bk': _L1_gnn_in['bk']}

def reference(x, adj, L0_gnn_weight, L0_gnn_bias, L1_gnn_rel_pair_index, L1_gnn_Wq, L1_gnn_bq, L1_gnn_Wk, L1_gnn_bk):
    import jax
    import jax.numpy as jnp

    def _L0_gnn_ref(x, adj, weight, bias):
        import jax, jax.numpy as jnp
        import numpy as np
        N = 4096
        IN_FEATURES = 512
        OUT_FEATURES = 512
        support = jnp.matmul(x, weight)
        output = jnp.matmul(adj, support)
        return output + bias

    def _L1_gnn_ref(inst_feature, aggregator_matrix, rel_pair_index, Wq, bq, Wk, bk):
        import jax, jax.numpy as jnp
        import numpy as np
        N, H, E, HEADS = (1500, 512, 10000, 8)
        DK = H // HEADS
        n = inst_feature.shape[0]
        sub = rel_pair_index[:, 0]
        obj = rel_pair_index[:, 1]
        q = (inst_feature[sub] @ Wq.T + bq).reshape(-1, HEADS, DK)
        k = (inst_feature[obj] @ Wk.T + bk).reshape(-1, HEADS, DK)
        att = ((q * k).sum(-1) / np.sqrt(DK)).T.astype(inst_feature.dtype)
        scores = jnp.zeros((HEADS, n, n), dtype=inst_feature.dtype)
        scores = scores.at[:, sub, obj].set(att)
        mask = (1.0 - aggregator_matrix).astype(bool)
        scores = jnp.where(mask[None], -jnp.inf, scores)
        di = jnp.arange(n)
        scores = scores.at[:, di, di].set(1e-07)
        attn = jax.nn.softmax(scores, axis=2)
        aggregator_factor = attn.sum(axis=0) / HEADS
        return aggregator_factor @ inst_feature
    h = jnp.maximum(_layernorm(x, axis=-1), 0.0)
    x = x + _L0_gnn_ref(h, adj, L0_gnn_weight, L0_gnn_bias)
    h = jnp.maximum(_layernorm(x, axis=-1), 0.0)
    x = x + _L1_gnn_ref(h, adj, L1_gnn_rel_pair_index, L1_gnn_Wq, L1_gnn_bq, L1_gnn_Wk, L1_gnn_bk)
    return x

_drawn_inputs = setup_inputs


def setup_inputs(seed=0):
    import zlib

    import numpy as np

    out = dict(_drawn_inputs(seed))
    spreads = {'L1_gnn_bq': (0.0, 0.1), 'L1_gnn_bk': (0.0, 0.1)}
    factors = {'L0_gnn_bias': 8.0}
    for name, (base, spread) in spreads.items():
        noise = np.random.default_rng([zlib.crc32(name.encode()), seed]).standard_normal(out[name].shape)
        drawn = base * np.exp(spread * noise) if base else spread * noise
        out[name] = jnp.asarray(drawn.astype(out[name].dtype))
    for name, factor in factors.items():
        out[name] = (out[name] * factor).astype(out[name].dtype)
    return out
```

```python
from contextlib import ExitStack

import concourse.bass as bass
from concourse import mybir

P = 128
BANK = 512
ALU = mybir.AluOpType
ACT = mybir.ActivationFunctionType
AX = mybir.AxisListType
F32 = mybir.dt.float32
F16 = mybir.dt.float16
BF16 = mybir.dt.bfloat16
I32 = mybir.dt.int32
U32 = mybir.dt.uint32

HEADS = 8
EPS = 1e-5
MASKED = 1e30
SELF_SCORE = 1e-7

W_SCALE = 64.0
H_SCALE = 8.0
ADJ_SCALE = 256.0
SUP_SCALE = 64.0


class Tile:

    def __init__(self, half, odd):
        self.half, self.odd = half, odd
        self.n = half * 2 + odd
        self.fixed = isinstance(half, int)

    def __add__(self, k):
        return Tile(self.half + (self.odd + k) // 2, (self.odd + k) % 2)

    def within(self, a, b):
        return not self.fixed or a <= self.n < b


def fixed(n):
    return Tile(n // 2, n % 2)


def over_tiles(eng, step, first, loop, tail, end):
    for n in range(first, loop):
        step(fixed(n))
    if tail > loop:
        with eng.Fori(loop // 2, tail // 2) as i:
            step(Tile(i, 0))
            step(Tile(i, 1))
    for n in range(tail, end):
        step(fixed(n))


def wait(eng, sem, count):
    if not isinstance(count, int) or count > 0:
        eng.wait_ge(sem, count)


def row_parts(rows):
    full = rows - rows % 16
    return [(a, b) for a, b in ((0, full), (full, rows)) if b > a]


def groups_of(blocks):
    n = -(-blocks // 4)
    n += n % 2
    sizes = [blocks // n + (k < blocks % n) for k in range(n)]
    return [(sum(sizes[:k]), sizes[k]) for k in range(n)]


def gnn_kernel(nc, x, adj, w0, b0, pairs, wq, bq, wk, bk, out):
    N, D = x.shape
    T = -(-N // P)
    LAST = N - (T - 1) * P
    assert D == BANK and T % 2 == 0 and T >= 12 and 96 < LAST < P

    with ExitStack() as ctx:
        def sb(name, shape, dt):
            return ctx.enter_context(nc.sbuf_tensor(name, shape, dt))

        NP = T * P
        mem = {
            "x1": sb("x1", [P, T, D], F32),
            "sup": sb("sup", [P, T * D], F32),
            "work": sb("work", [P, 4 * NP], F32),
            "ident": sb("ident", [P, P], F32),
            "ones": sb("ones", [P, 1], F32),
            "rstd": sb("rstd", [P, T], F32),
            "nmr": sb("nmr", [P, T], F32),
            "weights": sb("weights", [P, 8 * D], F32),
            "rows_out": sb("rows_out", [P, 2, D], F32),
            "h": sb("h", [P, 2, D], F32),
            "hT": sb("hT", [P, 4 * D], F16),
            "bias": sb("bias", [P, D], F32),
            "flag": sb("flag", [1, 1], I32),
        }
        banks = [ctx.enter_context(nc.psum_tensor(f"bank{k}", [P, BANK], F32)) for k in range(8)]
        layer0_and_diagonal(nc, mem, banks, x, adj, w0, b0, out)
        ones_found = nc.values_load(mem["flag"][0:1, 0:1], min_val=0, max_val=P * NP)
        with nc.If(ones_found > 0):
            attention_layer(nc, mem, banks, adj, pairs, wq, bq, wk, bk, out)


def layer0_and_diagonal(nc, mem, banks, x, adj, w0, b0, out):
    N, D = x.shape
    C = D // P
    T = -(-N // P)
    NP = T * P
    LAST = N - (T - 1) * P
    GROUPS = groups_of(T)
    G = len(GROUPS)
    FIRST, LOOP = -4, 2
    TAIL = T - 6
    EARLY = {}
    for g in range(G):
        EARLY.setdefault(TAIL + g * 6 // G, []).append(g)

    with ExitStack() as ctx:
        def sb(name, shape, dt):
            return ctx.enter_context(nc.sbuf_tensor(name, shape, dt))

        def sem(name):
            return ctx.enter_context(nc.semaphore(name))

        x1, ident, ones, bias = mem["x1"], mem["ident"], mem["ones"], mem["bias"]
        rstd, nmr, rows_out, h, flag = mem["rstd"], mem["nmr"], mem["rows_out"], mem["h"], mem["flag"]
        sup = [mem["sup"][:, k * T * D // 2:(k + 1) * T * D // 2].bitcast(F16)
               .rearrange("p (t d) -> p t d", d=D) for k in range(2)]
        sup_hi, sup_lo = sup
        work = mem["work"]
        adj_raw = [work[:, k * NP:(k + 1) * NP] for k in range(2)]
        at = [work[:, (2 + k) * NP:(3 + k) * NP].bitcast(F16) for k in range(2)]
        at_hi = [a[:, 0:NP] for a in at]
        at_lo = [a[:, NP:2 * NP] for a in at]
        w_raw = mem["weights"][:, 0:C * D].rearrange("p (c d) -> p c d", c=C)
        w_halves = mem["weights"][:, C * D:2 * C * D].bitcast(F16)
        w_hi = w_halves[:, 0:C * D].rearrange("p (c d) -> p c d", c=C)
        w_lo = w_halves[:, C * D:2 * C * D].rearrange("p (c d) -> p c d", c=C)
        hT_hi = mem["hT"][:, 0:2 * D].rearrange("p (k d) -> p k d", k=2)
        hT_lo = mem["hT"][:, 2 * D:4 * D].rearrange("p (k d) -> p k d", k=2)
        bn6 = sb("bn6", [P, 2, 6], F32)
        mv = sb("mv", [P, 2, 2], F32)
        ve = sb("ve", [P, 2], F32)
        sd = sb("sd", [P, 2], F32)
        r0 = sb("r0", [P, 2], F32)
        r1 = sb("r1", [P, 2], F32)
        is_one = sb("is_one", [P, max(n for _, n in GROUPS) * P], BF16)
        ones_seen = sb("ones_seen", [P, T * G], F32)
        held = sb("held", [P, 1], F32)
        ones_of_row = sb("ones_of_row", [P, 1], F32)
        ps_hT, ps_sup, ps_adj, ps_acc = banks[0:2], banks[2:4], banks[4:6], banks[6:8]

        x_in = [sem(f"x_in{k}") for k in range(2)]
        adj_in = [sem(f"adj_in{k}") for k in range(2)]
        stored = [sem(f"stored{k}") for k in range(2)]
        w_in = sem("w_in")
        bias_in = sem("bias_in")
        padded = sem("padded")
        blank = sem("blank")
        ident_done = sem("ident_done")
        ones_done = sem("ones_done")
        w_hi_done = sem("w_hi_done")
        w_lo_done = sem("w_lo_done")
        linked = sem("linked")
        var_done = sem("var_done")
        root_done = sem("root_done")
        stat_done = sem("stat_done")
        h_done = sem("h_done")
        hT_done = sem("hT_done")
        hhi_done = sem("hhi_done")
        hlo_done = sem("hlo_done")
        sup_done = sem("sup_done")
        shi_done = sem("shi_done")
        slo_done = sem("slo_done")
        bias_added = sem("bias_added")
        adjT_done = sem("adjT_done")
        ahi_done = sem("ahi_done")
        alo_done = sem("alo_done")
        counted = sem("counted")
        acc_done = sem("acc_done")
        x1_done = sem("x1_done")
        h2_done = sem("h2_done")
        rows_done = sem("rows_done")
        row_ones = sem("row_ones")
        all_ones = sem("all_ones")
        flag_done = sem("flag_done")

        block = ctx.enter_context(nc.Block())

        def parts(t):
            return row_parts(LAST if t.fixed and t.n == T - 1 else P)

        @block.sync
        def _(sp):
            def load_x(t):
                wait(sp, x_in[t.odd], t.half * 16)
                if t.fixed and t.n == T - 1:
                    sp.wait_ge(padded, 1)
                for a, b in parts(t):
                    sp.dma_start(x1[a:b, t.n, :], x[bass.ds(t.n * P + a, b - a), :]).then_inc(x_in[t.odd], 16)

            load_x(fixed(0))
            load_x(fixed(1))
            sp.dma_start(w_raw, w0.rearrange("(c p) n -> p c n", p=P)).then_inc(w_in, 16)
            sp.dma_start(bias[:], b0.rearrange("(a d) -> a d", a=1).broadcast_to([P, D])).then_inc(bias_in, 16)
            over_tiles(sp, load_x, 2, 2, T - 2, T)

            def load_adj(t):
                wait(sp, adjT_done, (t.n - 1) * G)
                wait(sp, counted, (t.n - 1) * G)
                for a, b in parts(t):
                    sp.dma_start(adj_raw[t.odd][a:b, 0:N],
                                 adj[bass.ds(t.n * P + a, b - a), :]).then_inc(adj_in[t.odd], 16)

            def store(t):
                sp.wait_ge(rows_done, t.n + 1)
                for a, b in parts(t):
                    sp.dma_start(out[bass.ds(t.n * P + a, b - a), :],
                                 rows_out[a:b, t.odd, :]).then_inc(stored[t.odd], 16)

            load_adj(fixed(0))
            load_adj(fixed(1))

            def step(m):
                if m.within(0, T - 2):
                    load_adj(m + 2)
                if m.within(1, T):
                    store(m + -1)

            over_tiles(sp, step, 0, 2, T - 4, T)
            store(fixed(T - 1))
            sp.wait_ge(stored[0], 16 * (T // 2))
            sp.wait_ge(stored[1], 16 * (T // 2 - 1 + len(row_parts(LAST))))

        @block.gpsimd
        def _(pool):
            nc.gpsimd.memset(ident[:], 0.0).then_inc(blank, 1)
            pool.wait_ge(blank, 1)
            nc.gpsimd.affine_select(out=ident[:], in_=ident[:], compare_op=ALU.not_equal, fill=1.0, base=0,
                                    pattern=[[-1, P]], channel_multiplier=1).then_inc(ident_done, 1)
            pool.wait_ge(bias_in, 16)

            def add_bias(t):
                pool.wait_ge(h_done, t.n + 1)
                nc.gpsimd.tensor_tensor(x1[:, t.n, :], x1[:, t.n, :], bias[:], ALU.add).then_inc(bias_added, 1)

            def add_rows(t):
                pool.wait_ge(h2_done, t.n + 1)
                nc.gpsimd.tensor_tensor(rows_out[:, t.odd, :], rows_out[:, t.odd, :], x1[:, t.n, :],
                                        ALU.add).then_inc(rows_done, 1)

            over_tiles(pool, add_bias, 0, 0, T, T)
            over_tiles(pool, add_rows, 0, 0, T, T)

        @block.scalar
        def _(act):
            def root(n, count):
                act.wait_ge(var_done, count)
                nc.scalar.activation(sd[:, 0:n], ve[:, 0:n], ACT.Sqrt).then_inc(root_done, 1)

            def normalize(t):
                act.wait_ge(stat_done, t.half + 1)
                wait(act, hT_done, t.n - 1)
                nc.scalar.activation(h[:, t.odd, :], x1[:, t.n, :], ACT.Relu, bias=nmr[:, bass.ds(t.n, 1)],
                                     scale=rstd[:, bass.ds(t.n, 1)]).then_inc(h_done, 1)

            def h_high(t):
                act.wait_ge(hT_done, t.n + 1)
                wait(act, sup_done, t.n - 1)
                nc.scalar.activation(hT_hi[:, t.odd, :], ps_hT[t.odd][:], ACT.Copy,
                                     scale=H_SCALE).then_inc(hhi_done, 1)

            def sup_high(t):
                act.wait_ge(sup_done, t.n + 1)
                nc.scalar.activation(sup_hi[:, t.n, :], ps_sup[t.odd][:], ACT.Copy,
                                     scale=SUP_SCALE / (W_SCALE * H_SCALE)).then_inc(shi_done, 1)

            def adj_high(t, g):
                b, n = GROUPS[g]
                act.wait_ge(adjT_done, t.n * G + g + 1)
                nc.scalar.activation(at_hi[t.odd][:, b * P:(b + n) * P], ps_adj[g % 2][:, 0:n * P], ACT.Copy,
                                     scale=ADJ_SCALE).then_inc(ahi_done, 1)

            def step(s):
                if s.within(-2, T - 2):
                    normalize(s + 2)
                if s.within(-1, T - 1):
                    h_high(s + 1)
                if s.within(0, T):
                    sup_high(s)
                if s.odd == 0 and s.within(-4, T - 4):
                    root(2, s.half + 3)
                for g in EARLY.get(s.n, []) if s.fixed else []:
                    adj_high(fixed(0), g)
                if s.fixed and s.n == FIRST:
                    act.wait_ge(w_in, 16)
                    nc.scalar.activation(w_hi, w_raw, ACT.Copy, scale=W_SCALE).then_inc(w_hi_done, 1)

            over_tiles(act, step, FIRST, LOOP, TAIL, T)

            def normalize_x1(t):
                act.wait_ge(stat_done, T // 2 + t.n + 1)
                wait(act, stored[t.odd], t.half * 16)
                nc.scalar.activation(rows_out[:, t.odd, :], x1[:, t.n, :], ACT.Relu,
                                     bias=nmr[:, bass.ds(t.n, 1)],
                                     scale=rstd[:, bass.ds(t.n, 1)]).then_inc(h2_done, 1)

            def step2(m):
                for g in range(G):
                    if m.within(0, T - 1):
                        adj_high(m + 1, g)
                    if g == 1 and m.within(1, T):
                        root(1, (m + -1).n + T // 2 + 1)
                    if g == 3 and m.within(1, T):
                        normalize_x1(m + -1)

            over_tiles(act, step2, 0, 2, T - 2, T)
            root(1, T + T // 2)
            normalize_x1(fixed(T - 1))

        @block.vector
        def _(dve):
            def link(ins, count):
                ins.then_inc(linked, 1)
                dve.wait_ge(linked, count)

            def hold():
                nc.vector.memset(held[:], 0.0)

            def statistics(first, n, base):
                hold()
                for k in range(n):
                    ins = nc.vector.bn_stats(bn6[:, k, :], x1[:, first.n + k, :])
                link(ins, base + 1)
                hold()
                for k in range(n):
                    ins = nc.vector.bn_aggr(mv[:, k, :], bn6[:, k, :])
                link(ins, base + 2)
                nc.vector.tensor_scalar(ve[:, 0:n], mv[:, 0:n, 1], EPS, None, ALU.add).then_inc(var_done, 1)

            def scales(first, n, base, count):
                dve.wait_ge(root_done, count)
                link(nc.vector.reciprocal(r0[:, 0:n], sd[:, 0:n]), base + 3)
                link(nc.vector.tensor_tensor(r1[:, 0:n], r0[:, 0:n], r0[:, 0:n], ALU.mult), base + 4)
                link(nc.vector.tensor_tensor(r1[:, 0:n], r1[:, 0:n], ve[:, 0:n], ALU.mult), base + 5)
                link(nc.vector.tensor_scalar(r1[:, 0:n], r1[:, 0:n], -0.5, 1.5, ALU.mult, ALU.add), base + 6)
                link(nc.vector.tensor_tensor(rstd[:, bass.ds(first.n, n)], r0[:, 0:n], r1[:, 0:n], ALU.mult),
                     base + 7)
                nc.vector.scalar_tensor_tensor(out=nmr[:, bass.ds(first.n, n)], in0=mv[:, 0:n, 0], scalar=-1.0,
                                               in1=rstd[:, bass.ds(first.n, n)], op0=ALU.mult,
                                               op1=ALU.mult).then_inc(stat_done, 1)

            LINKS = 7

            nc.vector.memset(x1[96:P, T - 1, :], 0.0)
            for k in range(2):
                ins = nc.vector.memset(adj_raw[k][:, N:NP], 0.0)
            ins.then_inc(padded, 1)
            nc.vector.memset(ones[:], 1.0).then_inc(ones_done, 1)

            def h_low(t):
                dve.wait_ge(hhi_done, t.n + 1)
                nc.vector.scalar_tensor_tensor(out=hT_lo[:, t.odd, :], in0=ps_hT[t.odd][:], scalar=H_SCALE,
                                               in1=hT_hi[:, t.odd, :], op0=ALU.mult,
                                               op1=ALU.subtract).then_inc(hlo_done, 1)

            def sup_low(t):
                dve.wait_ge(shi_done, t.n + 1)
                nc.vector.scalar_tensor_tensor(out=sup_lo[:, t.n, :], in0=ps_sup[t.odd][:],
                                               scalar=SUP_SCALE / (W_SCALE * H_SCALE), in1=sup_hi[:, t.n, :],
                                               op0=ALU.mult, op1=ALU.subtract).then_inc(slo_done, 1)

            def adj_low(t, g):
                b, n = GROUPS[g]
                dve.wait_ge(ahi_done, t.n * G + g + 1)
                nc.vector.scalar_tensor_tensor(out=at_lo[t.odd][:, b * P:(b + n) * P], in0=ps_adj[g % 2][:, 0:n * P],
                                               scalar=ADJ_SCALE, in1=at_hi[t.odd][:, b * P:(b + n) * P],
                                               op0=ALU.mult, op1=ALU.subtract).then_inc(alo_done, 1)
                wait(dve, counted, t.n * G + g)
                nc.vector.tensor_scalar(is_one[:, 0:n * P], adj_raw[t.odd][:, b * P:(b + n) * P], 1.0, 0.0,
                                        ALU.is_equal, ALU.add,
                                        accum_out=ones_seen[:, bass.ds(t.n * G + g, 1)]).then_inc(counted, 1)

            def step(s):
                if s.odd == 0 and s.within(-4, T - 4):
                    pair = s + 4
                    dve.wait_ge(x_in[0], 16 * pair.half + 16)
                    dve.wait_ge(x_in[1], 16 * (pair.half + 1) if not (pair.fixed and pair.n == T - 2)
                                else 16 * (pair.half + len(row_parts(LAST))))
                    statistics(pair, 2, pair.half * LINKS)
                if s.within(-1, T - 1):
                    h_low(s + 1)
                if s.within(0, T):
                    sup_low(s)
                if s.odd == 1 and s.within(-3, T - 3):
                    pair = s + 3
                    scales(pair, 2, pair.half * LINKS, pair.half + 1)
                for g in EARLY.get(s.n, []) if s.fixed else []:
                    adj_low(fixed(0), g)
                if s.fixed and s.n == FIRST:
                    dve.wait_ge(w_hi_done, 1)
                    nc.vector.scalar_tensor_tensor(out=w_lo, in0=w_raw, scalar=W_SCALE, in1=w_hi, op0=ALU.mult,
                                                   op1=ALU.subtract).then_inc(w_lo_done, 1)

            over_tiles(dve, step, FIRST, LOOP, TAIL, T)

            def links_before(t):
                return (t.n + T // 2) * LINKS

            def finish(t):
                dve.wait_ge(acc_done, t.n + 1)
                nc.vector.scalar_tensor_tensor(out=x1[:, t.n, :], in0=ps_acc[t.odd][:],
                                               scalar=1.0 / (ADJ_SCALE * SUP_SCALE), in1=x1[:, t.n, :],
                                               op0=ALU.mult, op1=ALU.add).then_inc(x1_done, 1)
                dve.wait_ge(x1_done, t.n + 1)
                statistics(t, 1, links_before(t))

            dve.wait_ge(bias_added, T)

            def step2(m):
                for g in range(G):
                    if m.within(0, T - 1):
                        adj_low(m + 1, g)
                    if g == 0 and m.within(1, T):
                        finish(m + -1)
                    if g == 2 and m.within(1, T):
                        t = m + -1
                        scales(t, 1, links_before(t), t.n + T // 2 + 1)
                if m.fixed and m.n == T - 2:
                    dve.wait_ge(counted, T * G)
                    nc.vector.tensor_reduce(ones_of_row[:], ones_seen[:], AX.X, ALU.add).then_inc(row_ones, 1)
                if m.fixed and m.n == T - 1:
                    dve.wait_ge(all_ones, 1)
                    nc.vector.tensor_copy(flag[0:1, 0:1], ps_adj[0][0:1, 0:1]).then_inc(flag_done, 1)

            over_tiles(dve, step2, 0, 2, T - 2, T)
            t = fixed(T - 1)
            finish(t)
            scales(t, 1, links_before(t), T + T // 2)

        @block.tensor
        def _(pe):
            def transpose_h(t):
                pe.wait_ge(h_done, t.n + 1)
                wait(pe, hlo_done, t.n - 1)
                for c in range(C):
                    mm = nc.tensor.transpose(ps_hT[t.odd][:, c * P:(c + 1) * P], h[:, t.odd, c * P:(c + 1) * P],
                                             ident[:])
                mm.then_inc(hT_done, 1)

            def times_w(t):
                pe.wait_ge(hlo_done, t.n + 1)
                wait(pe, slo_done, t.n - 1)
                for c in range(C):
                    hi, lo = (v[:, t.odd, c * P:(c + 1) * P] for v in (hT_hi, hT_lo))
                    nc.tensor.matmul(ps_sup[t.odd][:], hi, w_hi[:, c, :], start=(c == 0), stop=False)
                    nc.tensor.matmul(ps_sup[t.odd][:], hi, w_lo[:, c, :], start=False, stop=False)
                    mm = nc.tensor.matmul(ps_sup[t.odd][:], lo, w_hi[:, c, :], start=False, stop=(c == C - 1))
                mm.then_inc(sup_done, 1)

            def transpose_adj(t, g):
                b, n = GROUPS[g]
                if g == 0:
                    tiles = t.half + 1 if not (t.fixed and t.n == T - 1) else t.half + len(row_parts(LAST))
                    pe.wait_ge(adj_in[t.odd], tiles * 16)
                wait(pe, alo_done, t.n * G + g - 1)
                for k in range(n):
                    mm = nc.tensor.transpose(ps_adj[g % 2][:, k * P:(k + 1) * P],
                                             adj_raw[t.odd][:, (b + k) * P:(b + k + 1) * P], ident[:])
                mm.then_inc(adjT_done, 1)

            def times_support(t, g):
                b, n = GROUPS[g]
                if g == 0:
                    wait(pe, x1_done, t.n - 1)
                pe.wait_ge(alo_done, t.n * G + g + 1)
                for j in range(b, b + n):
                    hi, lo = (v[t.odd][:, j * P:(j + 1) * P] for v in (at_hi, at_lo))
                    nc.tensor.matmul(ps_acc[t.odd][:], hi, sup_hi[:, j, :], start=(j == 0), stop=False)
                    nc.tensor.matmul(ps_acc[t.odd][:], hi, sup_lo[:, j, :], start=False, stop=False)
                    mm = nc.tensor.matmul(ps_acc[t.odd][:], lo, sup_hi[:, j, :], start=False, stop=(j == T - 1))
                if g == G - 1:
                    mm.then_inc(acc_done, 1)

            pe.wait_ge(ident_done, 1)
            pe.wait_ge(padded, 1)

            def step(s):
                if s.within(-1, T - 1):
                    transpose_h(s + 1)
                if s.fixed and s.n == 0:
                    pe.wait_ge(w_lo_done, 1)
                if s.within(0, T):
                    times_w(s)
                for g in EARLY.get(s.n, []) if s.fixed else []:
                    transpose_adj(fixed(0), g)

            over_tiles(pe, step, FIRST, LOOP, TAIL, T)
            pe.wait_ge(slo_done, T)

            def step2(m):
                for g in range(G):
                    if m.within(0, T - 1):
                        transpose_adj(m + 1, g)
                    times_support(m, g)
                    if g == 0 and m.fixed and m.n == T - 1:
                        pe.wait_ge(ones_done, 1)
                        pe.wait_ge(row_ones, 1)
                        nc.tensor.matmul(ps_adj[0][0:1, 0:1], ones_of_row[:], ones[:], start=True,
                                         stop=True).then_inc(all_ones, 1)

            over_tiles(pe, step2, 0, 2, T - 2, T)


def attention_layer(nc, mem, banks, adj, pairs, wq, bq, wk, bk, out):
    N, D = out.shape
    C = D // P
    T = -(-N // P)
    NP = T * P
    LAST = N - (T - 1) * P
    DK = D // HEADS
    E = pairs.shape[0]
    EROWS = max(r for r in range(1, P + 1) if E % r == 0)
    ECOLS = E // EROWS
    COLS = [(c, min(BANK, NP - c)) for c in range(0, NP, BANK)]
    assert N * N < 1 << 24
    assert DK == 64

    with ExitStack() as ctx:
        def sb(name, shape, dt):
            return ctx.enter_context(nc.sbuf_tensor(name, shape, dt))

        def sem(name):
            return ctx.enter_context(nc.semaphore(name))

        x1, ident, ones = mem["x1"], mem["ident"], mem["ones"]
        rstd, nmr = mem["rstd"], mem["nmr"]
        h2 = mem["sup"][:].rearrange("p (t d) -> p t d", d=D)
        kT = mem["work"][:].rearrange("p (c n) -> p c n", c=C)
        wkT = mem["weights"][:, 0:C * D].rearrange("p (c d) -> p c d", c=C)
        wqT = mem["weights"][:, C * D:2 * C * D].rearrange("p (c d) -> p c d", c=C)
        w_rows = mem["rows_out"][:, 0, :]
        result = mem["rows_out"][:, 1, :]
        h2_tile = mem["h"][:, 0, :]
        x1_tile = mem["h"][:, 1, :]
        h2T = mem["hT"][:, 0:2 * D].bitcast(F32)
        qT = mem["hT"][:, 2 * D:4 * D].bitcast(F32)
        wide = [x1[:].rearrange("p t d -> p (t d)")[:, k * NP:(k + 1) * NP] for k in range(4)]
        bias_of, scale_of, score, factor = wide
        off_diag = mem["bias"][:, 0:P]
        diag = mem["bias"][:, P:2 * P]
        meanT = mem["bias"][:, 2 * P:3 * P]

        bqT = sb("bqT", [P, C], F32)
        bkT = sb("bkT", [P, C], F32)
        pair_ids = sb("pair_ids", [EROWS, ECOLS, 2], I32)
        places = sb("places", [EROWS, ECOLS], U32)
        place = sb("place", [EROWS, 1], U32)
        held = sb("held_scatter", [P, 1], F32)
        top = sb("top", [P, 1], F32)
        minus_top = sb("minus_top", [P, 1], F32)
        total = sb("total", [P, 1], F32)
        share = sb("share", [P, 1], F32)
        x1_dram = nc.dram_tensor("x1_rows", [N, D], F32).ap()
        listed_dram = nc.dram_tensor("listed_pairs", [N * N, 1], F32).ap()
        listed_rows = listed_dram.rearrange("(r c) a -> r (c a)", c=N)

        ps_T, ps_P, ps_S, ps_M, ps_O = banks[0], banks[1], banks[2:4], banks[4], banks[5]

        small_in = sem("small_in")
        x1_saved = sem("x1_saved")
        w_rows_in = sem("w_rows_in")
        wT_done = sem("wT_done")
        wT_kept = sem("wT_kept")
        h2_made = sem("h2_made")
        h2_kept = sem("h2_kept")
        h2T_done = sem("h2T_done")
        h2T_kept = sem("h2T_kept")
        k_done = sem("k_done")
        k_kept = sem("k_kept")
        wide_clear = sem("wide_clear")
        zeros_stored = sem("zeros_stored")
        places_done = sem("places_done")
        place_done = sem("place_done")
        scattered = sem("scattered")
        diag_blank = sem("diag_blank")
        diag_done = sem("diag_done")
        tile_in = sem("tile_in")
        q_tile = sem("q_tile")
        qh_done = sem("qh_done")
        qh_kept = sem("qh_kept")
        q_done = sem("q_done")
        q_kept = sem("q_kept")
        chain = sem("chain")
        dots_done = sem("dots_done")
        dots_used = sem("dots_used")
        top_done = sem("top_done")
        exp_done = sem("exp_done")
        factor_done = sem("factor_done")
        meanT_done = sem("meanT_done")
        meanT_kept = sem("meanT_kept")
        mean_used = sem("mean_used")
        product_done = sem("product_done")
        result_done = sem("result_done")
        result_stored = sem("result_stored")

        LOADS = 3
        block = ctx.enter_context(nc.Block())

        @block.sync
        def _(sp):
            sp.dma_start(pair_ids[:], pairs.rearrange("(p c) k -> p c k", p=EROWS)).then_inc(small_in, 16)
            for k in range(C):
                sp.dma_start(bqT[:, k:k + 1], bq.rearrange("(c p a) -> c p a", p=P, a=1)[k]).then_inc(small_in, 16)
                sp.dma_start(bkT[:, k:k + 1], bk.rearrange("(c p a) -> c p a", p=P, a=1)[k]).then_inc(small_in, 16)
            sp.dma_start(x1_dram[0:(T - 1) * P, :].rearrange("(t p) d -> p t d", p=P),
                         x1[:, 0:T - 1, :]).then_inc(x1_saved, 16)
            sp.dma_start(x1_dram[(T - 1) * P:N, :], x1[0:LAST, T - 1, :]).then_inc(x1_saved, 16)
            for n in range(2 * C):
                w = wk if n < C else wq
                wait(sp, wT_done, n)
                sp.dma_start(w_rows, w[(n % C) * P:(n % C + 1) * P, :]).then_inc(w_rows_in, 16)

            sp.wait_ge(wide_clear, 1)
            with sp.Fori(0, T - 1) as t:
                sp.dma_start(listed_rows[bass.ds(t * P, P), :], score[:, 0:N]).then_inc(zeros_stored, 16)
            sp.dma_start(listed_rows[(T - 1) * P:N, :], score[0:LAST, 0:N]).then_inc(zeros_stored, 16)
            sp.wait_ge(zeros_stored, 16 * T)
            sp.wait_ge(scattered, 16 * ECOLS)

            def tile(t, rows):
                wait(sp, result_done, t)
                for a, b in row_parts(rows):
                    at = bass.ds(t * P + a, b - a)
                    sp.dma_start(bias_of[a:b, 0:N], adj[at, :]).then_inc(tile_in, 16)
                    sp.dma_start(scale_of[a:b, 0:N], listed_rows[at, :]).then_inc(tile_in, 16)
                    sp.dma_start(x1_tile[a:b, :], x1_dram[at, :]).then_inc(tile_in, 16)
                sp.wait_ge(result_done, t + 1)
                for a, b in row_parts(rows):
                    sp.dma_start(out[bass.ds(t * P + a, b - a), :], result[a:b, :]).then_inc(result_stored, 16)

            tile(0, P)
            with sp.Fori(1, T - 1) as t:
                tile(t, P)
            tile(T - 1, LAST)
            sp.wait_ge(result_stored, 16 * (T - 1 + len(row_parts(LAST))))

        @block.gpsimd
        def _(pool):
            nc.gpsimd.memset(off_diag, 1.0)
            nc.gpsimd.memset(diag, 0.0).then_inc(diag_blank, 1)
            pool.wait_ge(diag_blank, 1)
            for block_, fill in ((off_diag, 0.0), (diag, SELF_SCORE)):
                ins = nc.gpsimd.affine_select(out=block_, in_=block_, compare_op=ALU.not_equal, fill=fill, base=0,
                                              pattern=[[-1, P]], channel_multiplier=1)
            ins.then_inc(diag_done, 1)

            pool.wait_ge(places_done, 1)
            pool.wait_ge(zeros_stored, 16 * T)

            def scatter(j):
                wait(pool, scattered, j * 16)
                nc.gpsimd.tensor_copy(place[:], places[:, bass.ds(j, 1)]).then_inc(place_done, 1)
                pool.wait_ge(place_done, j + 1)
                nc.gpsimd.tensor_tensor(held[:], ones[:], ones[:], ALU.mult)
                nc.gpsimd.indirect_dma_start(out=listed_dram, in_=ones[0:EROWS, :], in_offset=None,
                                             out_offset=bass.IndirectOffsetOnAxis(ap=place[:], axis=0)
                                             ).then_inc(scattered, 16)

            scatter(0)
            if ECOLS > 1:
                with pool.Fori(1, ECOLS) as j:
                    scatter(j)

        @block.scalar
        def _(act):
            def make_h2(t):
                wait(act, h2T_done, t)
                wait(act, h2_kept, t)
                nc.scalar.activation(h2_tile, x1[:, t, :], ACT.Relu, bias=nmr[:, bass.ds(t, 1)],
                                     scale=rstd[:, bass.ds(t, 1)]).then_inc(h2_made, 1)
                act.wait_ge(h2_made, t + 1)
                nc.scalar.activation(h2[:, t, :], h2_tile, ACT.Copy).then_inc(h2_kept, 1)

            make_h2(0)
            with act.Fori(1, T) as t:
                make_h2(t)

            def tile(t):
                act.wait_ge(qh_done, t)
                nc.scalar.activation(h2_tile, h2[:, t, :], ACT.Copy).then_inc(q_tile, 1)
                for head in range(HEADS):
                    act.wait_ge(top_done, t * HEADS + head + 1)
                    nc.scalar.activation(score[:, :], score[:, :], ACT.Exp, bias=minus_top[:], scale=1.0,
                                         accum_out=total[:]).then_inc(exp_done, 1)

            act.wait_ge(h2T_done, T)
            with act.Fori(0, T) as t:
                tile(t)

        @block.vector
        def _(dve):
            for n in range(2 * C):
                dve.wait_ge(wT_done, n + 1)
                wT, oc = (wkT, n) if n < C else (wqT, n - C)
                nc.vector.tensor_copy(wT[:, :, oc * P:(oc + 1) * P],
                                      ps_T[:].rearrange("p (c n) -> p c n", c=C)).then_inc(wT_kept, 1)
            dve.wait_ge(small_in, 16 * (1 + 2 * C))
            nc.vector.scalar_tensor_tensor(out=places[:], in0=pair_ids[:, :, 0], scalar=float(N),
                                           in1=pair_ids[:, :, 1], op0=ALU.mult, op1=ALU.add).then_inc(places_done, 1)

            def keep_k(t):
                dve.wait_ge(h2T_done, t + 1)
                wait(dve, k_done, t)
                nc.vector.tensor_copy(h2T, ps_T[:]).then_inc(h2T_kept, 1)
                dve.wait_ge(k_done, t + 1)
                for c in range(C):
                    ins = nc.vector.tensor_scalar(kT[:, c, bass.ds(t * P, P)], ps_P[:, c * P:(c + 1) * P],
                                                  bkT[:, c:c + 1], None, ALU.add)
                ins.then_inc(k_kept, 1)

            keep_k(0)
            with dve.Fori(1, T) as t:
                keep_k(t)
            dve.wait_ge(x1_saved, 32)
            dve.wait_ge(h2_kept, T)
            nc.vector.memset(x1[:], 0.0).then_inc(wide_clear, 1)
            dve.wait_ge(zeros_stored, 16 * T)
            dve.wait_ge(diag_done, 1)

            LINKS = 5 + HEADS * 4

            def tile(t, loads):
                made = [0]

                def link(ins):
                    made[0] += 1
                    ins.then_inc(chain, 1)
                    dve.wait_ge(chain, t * LINKS + made[0])

                dve.wait_ge(qh_done, t + 1)
                wait(dve, q_done, t)
                nc.vector.tensor_copy(h2T, ps_T[:]).then_inc(qh_kept, 1)
                dve.wait_ge(q_done, t + 1)
                wait(dve, dots_done, t * HEADS * len(COLS))
                for c in range(C):
                    ins = nc.vector.tensor_scalar(qT[:, c * P:(c + 1) * P], ps_P[:, c * P:(c + 1) * P],
                                                  bqT[:, c:c + 1], None, ALU.add)
                ins.then_inc(q_kept, 1)

                dve.wait_ge(tile_in, loads)
                link(nc.vector.tensor_scalar(bias_of, bias_of, 1.0, None, ALU.is_equal))
                link(nc.vector.scalar_tensor_tensor(out=scale_of, in0=scale_of, scalar=float(DK) ** -0.5,
                                                    in1=bias_of, op0=ALU.mult, op1=ALU.mult))
                link(nc.vector.tensor_scalar(bias_of, bias_of, -1.0, MASKED, ALU.add, ALU.mult))
                here = bass.ds(t * P, P)
                nc.vector.tensor_tensor(scale_of[:, here], scale_of[:, here], off_diag, ALU.mult)
                link(nc.vector.tensor_tensor(bias_of[:, here], bias_of[:, here], off_diag, ALU.mult))
                link(nc.vector.tensor_tensor(bias_of[:, here], bias_of[:, here], diag, ALU.add))

                for head in range(HEADS):
                    for k, (c, n) in enumerate(COLS):
                        dve.wait_ge(dots_done, (t * HEADS + head) * len(COLS) + k + 1)
                        ins = nc.vector.tensor_tensor(score[:, c:c + n], ps_S[k % 2][:, 0:n], scale_of[:, c:c + n],
                                                      ALU.mult)
                        ins.then_inc(dots_used, 1)
                    dve.wait_ge(dots_used, (t * HEADS + head + 1) * len(COLS))
                    link(nc.vector.tensor_tensor(score, score, bias_of, ALU.add))
                    link(nc.vector.tensor_reduce(top[:], score, AX.X, ALU.max))
                    nc.vector.tensor_scalar(minus_top[:], top[:], -1.0, None, ALU.mult).then_inc(top_done, 1)
                    dve.wait_ge(exp_done, t * HEADS + head + 1)
                    link(nc.vector.reciprocal(share[:], total[:]))
                    link(nc.vector.tensor_scalar(share[:], share[:], 1.0 / HEADS, None, ALU.mult))
                    if head == 0:
                        ins = nc.vector.tensor_scalar(factor, score, share[:], None, ALU.mult)
                    else:
                        ins = nc.vector.scalar_tensor_tensor(out=factor, in0=score, scalar=share[:], in1=factor,
                                                             op0=ALU.mult, op1=ALU.add)
                    ins.then_inc(factor_done, 1)
                    dve.wait_ge(factor_done, t * HEADS + head + 1)

                for j in range(T):
                    dve.wait_ge(meanT_done, t * T + j + 1)
                    wait(dve, mean_used, t * T + j)
                    nc.vector.tensor_copy(meanT, ps_M[:, 0:P]).then_inc(meanT_kept, 1)
                dve.wait_ge(mean_used, (t + 1) * T)
                wait(dve, result_stored, t * 16)
                nc.vector.tensor_tensor(result, ps_O[:], x1_tile, ALU.add).then_inc(result_done, 1)

            tile(0, 16 * LOADS)
            with dve.Fori(1, T - 1) as t:
                tile(t, (t + 1) * 16 * LOADS)
            tile(T - 1, 16 * LOADS * (T - 1 + len(row_parts(LAST))))

        @block.tensor
        def _(pe):
            for n in range(2 * C):
                pe.wait_ge(w_rows_in, 16 * (n + 1))
                wait(pe, wT_kept, n)
                for c in range(C):
                    mm = nc.tensor.transpose(ps_T[:, c * P:(c + 1) * P], w_rows[:, c * P:(c + 1) * P], ident[:])
                mm.then_inc(wT_done, 1)
            pe.wait_ge(wT_kept, 2 * C)

            def transpose_h2(done):
                for c in range(C):
                    mm = nc.tensor.transpose(ps_T[:, c * P:(c + 1) * P], h2_tile[:, c * P:(c + 1) * P], ident[:])
                mm.then_inc(done, 1)

            def project(wT, done):
                for c in range(C):
                    for k in range(C):
                        mm = nc.tensor.matmul(ps_P[:, c * P:(c + 1) * P], wT[:, k, c * P:(c + 1) * P],
                                              h2T[:, k * P:(k + 1) * P], start=(k == 0), stop=(k == C - 1))
                mm.then_inc(done, 1)

            def keys(t):
                pe.wait_ge(h2_made, t + 1)
                wait(pe, h2T_kept, t)
                transpose_h2(h2T_done)
                pe.wait_ge(h2T_kept, t + 1)
                wait(pe, k_kept, t)
                project(wkT, k_done)

            keys(0)
            with pe.Fori(1, T) as t:
                keys(t)
            pe.wait_ge(k_kept, T)
            pe.wait_ge(h2_kept, T)

            def tile(t):
                pe.wait_ge(q_tile, t + 1)
                wait(pe, qh_kept, t)
                transpose_h2(qh_done)
                pe.wait_ge(qh_kept, t + 1)
                wait(pe, q_kept, t)
                project(wqT, q_done)
                pe.wait_ge(q_kept, t + 1)
                for head in range(HEADS):
                    c, lanes = head * DK // P, slice(head * DK % P, head * DK % P + DK)
                    for k, (col, n) in enumerate(COLS):
                        wait(pe, dots_used, (t * HEADS + head) * len(COLS) + k - 1)
                        nc.tensor.matmul(ps_S[k % 2][:, 0:n], qT[lanes, c * P:(c + 1) * P],
                                         kT[lanes, c, col:col + n], start=True, stop=True).then_inc(dots_done, 1)
                pe.wait_ge(factor_done, (t + 1) * HEADS)
                for j in range(T):
                    wait(pe, meanT_kept, t * T + j)
                    nc.tensor.transpose(ps_M[:, 0:P], factor[:, j * P:(j + 1) * P], ident[:]).then_inc(meanT_done, 1)
                    pe.wait_ge(meanT_kept, t * T + j + 1)
                    if j == 0:
                        wait(pe, result_done, t)
                    mm = nc.tensor.matmul(ps_O[:], meanT, h2[:, j, :], start=(j == 0), stop=(j == T - 1))
                    mm.then_inc(mean_used, 1)

            tile(0)
            with pe.Fori(1, T) as t:
                tile(t)


_INS = ['x', 'adj', 'L0_gnn_weight', 'L0_gnn_bias', 'L1_gnn_rel_pair_index', 'L1_gnn_Wq', 'L1_gnn_bq',
        'L1_gnn_Wk', 'L1_gnn_bk']


def kernel(**inputs):
    import numpy as _np
    import concourse.bacc as _bacc
    from concourse import mybir as _mybir
    from concourse.bass_utils import run_bass_kernel_spmd as _run

    nc = _bacc.Bacc("TRN2", target_bir_lowering=False, num_devices=1)
    arrays, args = {}, []
    for name in _INS:
        a = _np.ascontiguousarray(inputs[name])
        arrays[f"in_{name}_dram"] = a
        args.append(nc.dram_tensor(f"in_{name}_dram", a.shape, _mybir.dt.from_np(a.dtype), kind="ExternalInput").ap())
    args.append(nc.dram_tensor("out_0_dram", inputs['x'].shape, _mybir.dt.float32, kind="ExternalOutput").ap())
    gnn_kernel(nc, *args)
    r = _run(nc, [arrays], core_ids=[0])
    return r.results[0]["out_0_dram"]
```

```python
from contextlib import ExitStack

import concourse.bass as bass
from concourse import mybir

P = 128
Q = 32
QUADS = P // Q
BANK = 512
ALU = mybir.AluOpType
ACT = mybir.ActivationFunctionType
AX = mybir.AxisListType
F32 = mybir.dt.float32
F16 = mybir.dt.float16
BF16 = mybir.dt.bfloat16
I32 = mybir.dt.int32
U32 = mybir.dt.uint32

HEADS = 8
EPS = 1e-5
MASKED = 1e30
SELF_SCORE = 1e-7

W_SCALE = 64.0
H_SCALE = 8.0
ADJ_SCALE = 256.0
SUP_SCALE = 64.0


class Tile:

    def __init__(self, half, odd):
        self.half, self.odd = half, odd
        self.n = half * 2 + odd
        self.fixed = isinstance(half, int)

    def __add__(self, k):
        return Tile(self.half + (self.odd + k) // 2, (self.odd + k) % 2)

    def within(self, a, b):
        return not self.fixed or a <= self.n < b


def fixed(n):
    return Tile(n // 2, n % 2)


def over_tiles(eng, step, first, loop, tail, end):
    for n in range(first, loop):
        step(fixed(n))
    if tail > loop:
        with eng.Fori(loop // 2, tail // 2) as i:
            step(Tile(i, 0))
            step(Tile(i, 1))
    for n in range(tail, end):
        step(fixed(n))


def wait(eng, sem, count):
    if not isinstance(count, int) or count > 0:
        eng.wait_ge(sem, count)


def row_parts(rows):
    full = rows - rows % 16
    return [(a, b) for a, b in ((0, full), (full, rows)) if b > a]


def quad_parts(last, short):
    return [(q, a, b) for q in range(QUADS) for a, b in (row_parts(short) if last and q == QUADS - 1 else [(0, Q)])]


def dram_rows(tensor, first, rows, quads, stride, col, cols):
    width = tensor.shape[1]
    return bass.AP(tensor.tensor, first * width + col, [[width, rows], [stride * width, quads], [1, cols]])




def gnn_kernel(nc, x, adj, w0, b0, pairs, wq, bq, wk, bk, out):
    N, D = x.shape
    T = -(-N // P)
    NP = T * P
    assert D == BANK and T % 2 == 0 and T >= 16 and 0 < NP - N < Q

    with ExitStack() as ctx:
        def sb(name, shape, dt):
            return ctx.enter_context(nc.sbuf_tensor(name, shape, dt))

        mem = {
            "x1": sb("x1", [P, T, D], F32),
            "sup": sb("sup", [P, T * D], F32),
            "work": sb("work", [P, 4 * NP], F32),
            "ident": sb("ident", [P, P], F32),
            "ones": sb("ones", [P, 1], F32),
            "rstd": sb("rstd", [P, T], F32),
            "nmr": sb("nmr", [P, T], F32),
            "adjT": sb("adjT", [P, NP], F32),
            "weights": sb("weights", [P, 4 * D], F32),
            "rows_out": sb("rows_out", [P, 2, D], F32),
            "h": sb("h", [P, 2, D], F32),
            "hT": sb("hT", [P, 4 * D], F16),
            "bias": sb("bias", [P, D], F32),
            "flag": sb("flag", [1, 1], I32),
        }
        psum = ctx.enter_context(nc.psum_tensor("psum", [P, 8, BANK], F32))
        layer0_and_diagonal(nc, mem, psum, x, adj, w0, b0, out)
        ones_found = nc.values_load(mem["flag"][0:1, 0:1], min_val=0, max_val=P * NP)
        with nc.If(ones_found > 0):
            attention_layer(nc, mem, psum, adj, pairs, wq, bq, wk, bk, out)


def layer0_and_diagonal(nc, mem, psum, x, adj, w0, b0, out):
    N, D = x.shape
    C = D // P
    T = -(-N // P)
    NP = T * P
    QUARTER = NP // QUADS
    SHORT = Q - (NP - N)
    HALVES = 2
    CHUNKS = 4
    CUTS = [k * T // CHUNKS for k in range(CHUNKS + 1)]
    S_STEPS = (-6, 2, T - 8, T + 1)
    M_STEPS = (-1, 2, T - 4, T)

    with ExitStack() as ctx:
        def sb(name, shape, dt):
            return ctx.enter_context(nc.sbuf_tensor(name, shape, dt))

        def sem(name):
            return ctx.enter_context(nc.semaphore(name))

        x1, ident, ones, bias = mem["x1"], mem["ident"], mem["ones"], mem["bias"]
        rstd, nmr, rows_out, h, flag = mem["rstd"], mem["nmr"], mem["rows_out"], mem["h"], mem["flag"]
        sup = [mem["sup"][:, k * T * D // 2:(k + 1) * T * D // 2].bitcast(F16)
               .rearrange("p (t d) -> p t d", d=D) for k in range(2)]
        sup_hi, sup_lo = sup
        work = mem["work"]
        adj_raw = [work[:, k * NP:(k + 1) * NP] for k in range(2)]
        at = [work[:, (2 + k) * NP:(3 + k) * NP].bitcast(F16) for k in range(2)]
        at_hi = [a[:, 0:NP] for a in at]
        at_lo = [a[:, NP:2 * NP] for a in at]
        adjT = mem["adjT"]
        w_raw = work[:, 3 * NP:3 * NP + C * D].rearrange("p (c d) -> p c d", c=C)
        w_halves = mem["weights"][:].bitcast(F16)
        w_hi = w_halves[:, 0:C * D].rearrange("p (c d) -> p c d", c=C)
        w_lo = w_halves[:, C * D:2 * C * D].rearrange("p (c d) -> p c d", c=C)
        hT_hi = mem["hT"][:, 0:2 * D].rearrange("p (k d) -> p k d", k=2)
        hT_lo = mem["hT"][:, 2 * D:4 * D].rearrange("p (k d) -> p k d", k=2)
        bn6 = sb("bn6", [P, 2, 6], F32)
        mv = sb("mv", [P, 2, 2], F32)
        ve = sb("ve", [P, 2], F32)
        sd = sb("sd", [P, 2], F32)
        r0 = sb("r0", [P, 2], F32)
        r1 = sb("r1", [P, 2], F32)
        ones_seen = sb("ones_seen", [P, T * HALVES], F32)
        held = sb("held", [P, 1], F32)
        ones_of_row = sb("ones_of_row", [P, 1], F32)
        ps_hT, ps_sup, ps_acc = ([psum[:, b + k, :] for k in range(2)] for b in (0, 2, 4))
        ps_flag = psum[0:1, 6, 0:1]
        is_one = psum[:, 0:4, :].rearrange("p b n -> p (b n)")[:, 0:NP // HALVES]

        x_in = [sem(f"x_in{q}") for q in range(QUADS)]
        adj_in = [sem(f"adj_in{k}") for k in range(2)]
        stored = [sem(f"stored{k}") for k in range(2)]
        w_in = sem("w_in")
        bias_in = sem("bias_in")
        padded = sem("padded")
        blank = sem("blank")
        ident_done = sem("ident_done")
        ones_done = sem("ones_done")
        w_hi_done = sem("w_hi_done")
        w_lo_done = sem("w_lo_done")
        linked = sem("linked")
        var_done = sem("var_done")
        root_done = sem("root_done")
        stat_done = sem("stat_done")
        h_done = sem("h_done")
        hT_done = sem("hT_done")
        hhi_done = sem("hhi_done")
        hlo_done = sem("hlo_done")
        sup_done = sem("sup_done")
        shi_done = sem("shi_done")
        slo_done = sem("slo_done")
        bias_added = sem("bias_added")
        adjT_done = sem("adjT_done")
        ahi_done = sem("ahi_done")
        alo_done = sem("alo_done")
        counted = sem("counted")
        acc_done = sem("acc_done")
        x1_done = sem("x1_done")
        h2_done = sem("h2_done")
        rows_done = sem("rows_done")
        row_ones = sem("row_ones")
        all_ones = sem("all_ones")
        flag_done = sem("flag_done")

        block = ctx.enter_context(nc.Block())

        def last(t):
            return t.fixed and t.n == T - 1

        def adj_parts(t):
            if not last(t):
                return [(q, 0, QUADS, 0, Q) for q in range(QUADS)]
            return [(q, first, n, a, b) for q in range(QUADS)
                    for first, n, a, b in [(0, QUADS - 1, 0, Q)] + [(QUADS - 1, 1, a, b) for a, b in row_parts(SHORT)]]

        def made(t):
            return t.n + CHUNKS

        def adj_landed(t):
            before = t.half * 16 * QUADS
            return before + 16 * len(adj_parts(t))

        @block.sync
        def _(sp):
            def load_x(t):
                for q in range(QUADS):
                    wait(sp, x_in[q], t.half * 16)
                    here = x[bass.ds(q * QUARTER + t.n * Q, 2 * Q), :] if not (last(t + 1) and q == QUADS - 1) else None
                    if here is not None:
                        sp.dma_start(x1[q * Q:(q + 1) * Q, bass.ds(t.n, 2), :],
                                     here.rearrange("(t i) d -> i t d", i=Q)).then_inc(x_in[q], 16)
                        continue
                    sp.wait_ge(padded, 1)
                    for tile, a, b in [(t.n, 0, Q)] + [(t.n + 1, a, b) for a, b in row_parts(SHORT)]:
                        first = q * QUARTER + tile * Q
                        sp.dma_start(x1[q * Q + a:q * Q + b, tile, :],
                                     x[first + a:first + b, :]).then_inc(x_in[q], 16)

            load_x(fixed(0))
            sp.dma_start(bias[:], b0.rearrange("(a d) -> a d", a=1).broadcast_to([P, D])).then_inc(bias_in, 16)
            with sp.Fori(1, T // 2 - 1) as i:
                load_x(Tile(i, 0))
            load_x(fixed(T - 2))

            def load_adj(t):
                for q, first, n, a, b in adj_parts(t):
                    cols = QUARTER if q < QUADS - 1 else N - q * QUARTER
                    dst = adj_raw[t.odd].rearrange("p (r c) -> p r c", r=QUADS)[q * Q + a:q * Q + b,
                                                                                 first:first + n, 0:cols]
                    sp.dma_start(dst, dram_rows(adj, first * QUARTER + t.n * Q + a, b - a, n, QUARTER,
                                                q * QUARTER, cols)).then_inc(adj_in[t.odd], 16)

            def store(t):
                sp.wait_ge(rows_done, t.n + 1)
                for q, a, b in quad_parts(last(t), SHORT):
                    sp.dma_start(out[bass.ds(q * QUARTER + t.n * Q + a, b - a), :],
                                 rows_out[q * Q + a:q * Q + b, t.odd, :]).then_inc(stored[t.odd], 16)

            sp.wait_ge(padded, 1)
            load_adj(fixed(0))
            load_adj(fixed(1))

            def step(m):
                if m.within(-1, T - 3):
                    sp.wait_ge(counted, (m.n + 2) * HALVES)
                    load_adj(m + 3)
                if m.within(1, T):
                    store(m + -1)

            over_tiles(sp, step, *M_STEPS)
            store(fixed(T - 1))
            sp.wait_ge(stored[0], 16 * QUADS * (T // 2))
            sp.wait_ge(stored[1], 16 * (QUADS * (T // 2 - 1) + len(quad_parts(True, SHORT))))

        @block.gpsimd
        def _(pool):
            nc.gpsimd.memset(ident[:], 0.0).then_inc(blank, 1)
            pool.wait_ge(blank, 1)
            nc.gpsimd.affine_select(out=ident[:], in_=ident[:], compare_op=ALU.not_equal, fill=1.0, base=0,
                                    pattern=[[-1, P]], channel_multiplier=1).then_inc(ident_done, 1)
            pool.wait_ge(bias_in, 16)

            def add_bias(t):
                pool.wait_ge(h_done, t.n + 1)
                nc.gpsimd.tensor_tensor(x1[:, t.n, :], x1[:, t.n, :], bias[:], ALU.add).then_inc(bias_added, 1)

            def add_rows(t):
                pool.wait_ge(h2_done, t.n + 1)
                nc.gpsimd.tensor_tensor(rows_out[:, t.odd, :], rows_out[:, t.odd, :], x1[:, t.n, :],
                                        ALU.add).then_inc(rows_done, 1)

            over_tiles(pool, add_bias, 0, 0, T, T)
            over_tiles(pool, add_rows, 0, 0, T, T)

        @block.scalar
        def _(act):
            act.dma_start(w_raw, w0.rearrange("(c p) n -> p c n", p=P)).then_inc(w_in, 16)

            def root(n, count):
                act.wait_ge(var_done, count)
                nc.scalar.activation(sd[:, 0:n], ve[:, 0:n], ACT.Sqrt).then_inc(root_done, 1)

            def normalize(t):
                act.wait_ge(stat_done, t.half + 1)
                wait(act, hT_done, t.n - 1)
                nc.scalar.activation(h[:, t.odd, :], x1[:, t.n, :], ACT.Relu, bias=nmr[:, bass.ds(t.n, 1)],
                                     scale=rstd[:, bass.ds(t.n, 1)]).then_inc(h_done, 1)

            def h_high(t):
                act.wait_ge(hT_done, t.n + 1)
                wait(act, sup_done, t.n - 1)
                nc.scalar.activation(hT_hi[:, t.odd, :], ps_hT[t.odd], ACT.Copy,
                                     scale=H_SCALE).then_inc(hhi_done, 1)

            def sup_high(t):
                act.wait_ge(sup_done, t.n + 1)
                nc.scalar.activation(sup_hi[:, t.n, :], ps_sup[t.odd], ACT.Copy,
                                     scale=SUP_SCALE / (W_SCALE * H_SCALE)).then_inc(shi_done, 1)

            def adj_high(t):
                act.wait_ge(adjT_done, made(t))
                wait(act, acc_done, t.n - 1)
                nc.scalar.activation(at_hi[t.odd], adjT[:], ACT.Copy, scale=ADJ_SCALE).then_inc(ahi_done, 1)

            def adj_high_chunk(k):
                cols = slice(CUTS[k] * P, CUTS[k + 1] * P)
                act.wait_ge(adjT_done, k + 1)
                nc.scalar.activation(at_hi[0][:, cols], adjT[:, cols], ACT.Copy, scale=ADJ_SCALE).then_inc(ahi_done, 1)

            def step(s):
                if s.within(-1, T - 1):
                    h_high(s + 1)
                if s.odd == 0 and s.within(-4, T - 4):
                    root(2, s.half + 3)
                if s.within(1, T + 1):
                    sup_high(s + -1)
                if s.within(-3, T - 3):
                    normalize(s + 3)
                if s.fixed and s.n == -1:
                    act.wait_ge(w_in, 16)
                    for c in range(C):
                        nc.scalar.activation(w_hi[:, c, :], w_raw[:, c, :], ACT.Copy,
                                             scale=W_SCALE).then_inc(w_hi_done, 1)
                if s.fixed and T - 4 <= s.n < T:
                    adj_high_chunk(s.n - (T - 4))

            over_tiles(act, step, *S_STEPS)

            def normalize_x1(t):
                act.wait_ge(stat_done, T // 2 + t.n + 1)
                wait(act, stored[t.odd], t.half * 16 * QUADS)
                nc.scalar.activation(rows_out[:, t.odd, :], x1[:, t.n, :], ACT.Relu,
                                     bias=nmr[:, bass.ds(t.n, 1)],
                                     scale=rstd[:, bass.ds(t.n, 1)]).then_inc(h2_done, 1)

            def step2(m):
                if m.within(0, T - 1):
                    adj_high(m + 1)
                if m.within(1, T):
                    root(1, (m + -1).n + T // 2 + 1)
                    normalize_x1(m + -1)

            over_tiles(act, step2, *M_STEPS)
            root(1, T + T // 2)
            normalize_x1(fixed(T - 1))

        @block.vector
        def _(dve):
            def link(ins, count):
                ins.then_inc(linked, 1)
                dve.wait_ge(linked, count)

            def hold():
                nc.vector.memset(held[:], 0.0)

            def spread(t, k):
                if k == 0:
                    hold()
                return nc.vector.bn_stats(bn6[:, k, :], x1[:, t.n, :])

            def variances(ins, n, base):
                link(ins, base + 1)
                hold()
                for k in range(n):
                    ins = nc.vector.bn_aggr(mv[:, k, :], bn6[:, k, :])
                link(ins, base + 2)
                nc.vector.tensor_scalar(ve[:, 0:n], mv[:, 0:n, 1], EPS, None, ALU.add).then_inc(var_done, 1)

            def scales(first, n, base, count):
                dve.wait_ge(root_done, count)
                link(nc.vector.reciprocal(r0[:, 0:n], sd[:, 0:n]), base + 3)
                link(nc.vector.tensor_tensor(r1[:, 0:n], r0[:, 0:n], r0[:, 0:n], ALU.mult), base + 4)
                link(nc.vector.tensor_tensor(r1[:, 0:n], r1[:, 0:n], ve[:, 0:n], ALU.mult), base + 5)
                link(nc.vector.tensor_scalar(r1[:, 0:n], r1[:, 0:n], -0.5, 1.5, ALU.mult, ALU.add), base + 6)
                link(nc.vector.tensor_tensor(rstd[:, bass.ds(first.n, n)], r0[:, 0:n], r1[:, 0:n], ALU.mult),
                     base + 7)
                nc.vector.scalar_tensor_tensor(out=nmr[:, bass.ds(first.n, n)], in0=mv[:, 0:n, 0], scalar=-1.0,
                                               in1=rstd[:, bass.ds(first.n, n)], op0=ALU.mult,
                                               op1=ALU.mult).then_inc(stat_done, 1)

            LINKS = 7

            nc.vector.memset(x1[P - Q:P, T - 1, :], 0.0)
            for k in range(2):
                padding = adj_raw[k].rearrange("p (r c) -> p r c", r=QUADS)[P - Q:P, :, QUARTER - (NP - N):QUARTER]
                ins = nc.vector.memset(padding, 0.0)
            ins.then_inc(padded, 1)
            nc.vector.memset(ones[:], 1.0).then_inc(ones_done, 1)

            def h_low(t):
                dve.wait_ge(hhi_done, t.n + 1)
                nc.vector.scalar_tensor_tensor(out=hT_lo[:, t.odd, :], in0=ps_hT[t.odd], scalar=H_SCALE,
                                               in1=hT_hi[:, t.odd, :], op0=ALU.mult,
                                               op1=ALU.subtract).then_inc(hlo_done, 1)

            def sup_low(t):
                dve.wait_ge(shi_done, t.n + 1)
                nc.vector.scalar_tensor_tensor(out=sup_lo[:, t.n, :], in0=ps_sup[t.odd],
                                               scalar=SUP_SCALE / (W_SCALE * H_SCALE), in1=sup_hi[:, t.n, :],
                                               op0=ALU.mult, op1=ALU.subtract).then_inc(slo_done, 1)

            def transpose_adj(t, lo, hi):
                src = adj_raw[t.odd].rearrange("p (r b j) -> p r b j", r=QUADS, j=Q)
                dst = adjT[:].rearrange("p (b r i) -> p r b i", r=QUADS, i=Q)
                nc.vector.transpose(dst[:, :, lo:hi, :], src[:, :, lo:hi, :]).then_inc(adjT_done, 1)

            def adj_low(t):
                dve.wait_ge(ahi_done, made(t))
                nc.vector.scalar_tensor_tensor(out=at_lo[t.odd], in0=adjT[:], scalar=ADJ_SCALE, in1=at_hi[t.odd],
                                               op0=ALU.mult, op1=ALU.subtract).then_inc(alo_done, 1)

            def adj_low_chunk(k):
                cols = slice(CUTS[k] * P, CUTS[k + 1] * P)
                dve.wait_ge(ahi_done, k + 1)
                nc.vector.scalar_tensor_tensor(out=at_lo[0][:, cols], in0=adjT[:, cols], scalar=ADJ_SCALE,
                                               in1=at_hi[0][:, cols], op0=ALU.mult,
                                               op1=ALU.subtract).then_inc(alo_done, 1)

            def count_ones(t):
                for k in range(HALVES):
                    wait(dve, counted, t.n * HALVES + k)
                    nc.vector.tensor_scalar(is_one, adj_raw[t.odd][:, k * NP // 2:(k + 1) * NP // 2], 1.0, 0.0,
                                            ALU.is_equal, ALU.add,
                                            accum_out=ones_seen[:, bass.ds(t.n * HALVES + k, 1)]
                                            ).then_inc(counted, 1)

            def step(s):
                if s.within(-1, T - 1):
                    h_low(s + 1)
                if s.within(1, T + 1):
                    sup_low(s + -1)
                t = s + 6
                if s.within(-6, T - 6):
                    if s.odd == 0:
                        for q in range(QUADS):
                            dmas = 1 if not (last(t + 1) and q == QUADS - 1) else 1 + len(row_parts(SHORT))
                            dve.wait_ge(x_in[q], 16 * (t.half + dmas))
                    ins = spread(t, s.odd)
                    if s.odd == 1:
                        variances(ins, 2, t.half * LINKS)
                if s.odd == 0 and s.within(-4, T - 4):
                    pair = s + 4
                    scales(pair, 2, pair.half * LINKS, pair.half + 1)
                if s.fixed and s.n == -1:
                    for c in range(C):
                        dve.wait_ge(w_hi_done, c + 1)
                        nc.vector.scalar_tensor_tensor(out=w_lo[:, c, :], in0=w_raw[:, c, :], scalar=W_SCALE,
                                                       in1=w_hi[:, c, :], op0=ALU.mult,
                                                       op1=ALU.subtract).then_inc(w_lo_done, 1)
                if s.fixed and s.n > T - 4:
                    adj_low_chunk(s.n - (T - 4) - 1)
                if s.fixed and T - 4 <= s.n < T:
                    k = s.n - (T - 4)
                    if k == 0:
                        dve.wait_ge(adj_in[0], adj_landed(fixed(0)))
                    transpose_adj(fixed(0), CUTS[k], CUTS[k + 1])

            over_tiles(dve, step, *S_STEPS)

            def links_before(t):
                return (t.n + T // 2) * LINKS

            def finish(t):
                dve.wait_ge(acc_done, t.n + 1)
                nc.vector.scalar_tensor_tensor(out=x1[:, t.n, :], in0=ps_acc[t.odd],
                                               scalar=1.0 / (ADJ_SCALE * SUP_SCALE), in1=x1[:, t.n, :],
                                               op0=ALU.mult, op1=ALU.add).then_inc(x1_done, 1)
                dve.wait_ge(x1_done, t.n + 1)
                variances(spread(t, 0), 1, links_before(t))

            dve.wait_ge(bias_added, T)
            dve.wait_ge(slo_done, T)

            def step2(m):
                if m.within(1, T):
                    finish(m + -1)
                if m.within(0, T - 1):
                    adj_low(m + 1)
                if m.within(1, T):
                    t = m + -1
                    scales(t, 1, links_before(t), t.n + T // 2 + 1)
                if m.fixed and m.n == -1:
                    count_ones(fixed(0))
                if m.within(-1, T - 2):
                    t = m + 2
                    dve.wait_ge(adj_in[t.odd], adj_landed(t))
                    dve.wait_ge(alo_done, made(t + -1))
                    transpose_adj(t, 0, T)
                    count_ones(t)
                if m.fixed and m.n == T - 2:
                    dve.wait_ge(counted, T * HALVES)
                    nc.vector.tensor_reduce(ones_of_row[:], ones_seen[:], AX.X, ALU.add).then_inc(row_ones, 1)
                if m.fixed and m.n == T - 1:
                    dve.wait_ge(all_ones, 1)
                    nc.vector.tensor_copy(flag[0:1, 0:1], ps_flag).then_inc(flag_done, 1)

            over_tiles(dve, step2, *M_STEPS)
            t = fixed(T - 1)
            finish(t)
            scales(t, 1, links_before(t), T + T // 2)

        @block.tensor
        def _(pe):
            def transpose_h(t):
                pe.wait_ge(h_done, t.n + 1)
                wait(pe, hlo_done, t.n - 1)
                for c in range(C):
                    mm = nc.tensor.transpose(ps_hT[t.odd][:, c * P:(c + 1) * P], h[:, t.odd, c * P:(c + 1) * P],
                                             ident[:])
                mm.then_inc(hT_done, 1)

            def times_w(t):
                pe.wait_ge(hlo_done, t.n + 1)
                wait(pe, slo_done, t.n - 1)
                for c in range(C):
                    if t.fixed and t.n == 0:
                        pe.wait_ge(w_lo_done, c + 1)
                    hi, lo = (v[:, t.odd, c * P:(c + 1) * P] for v in (hT_hi, hT_lo))
                    nc.tensor.matmul(ps_sup[t.odd], hi, w_hi[:, c, :], start=(c == 0), stop=False)
                    nc.tensor.matmul(ps_sup[t.odd], hi, w_lo[:, c, :], start=False, stop=False)
                    mm = nc.tensor.matmul(ps_sup[t.odd], lo, w_hi[:, c, :], start=False, stop=(c == C - 1))
                mm.then_inc(sup_done, 1)

            def times_support(t):
                wait(pe, x1_done, t.n - 1)
                pe.wait_ge(ahi_done, made(t))
                for j in range(T):
                    hi = at_hi[t.odd][:, j * P:(j + 1) * P]
                    nc.tensor.matmul(ps_acc[t.odd], hi, sup_hi[:, j, :], start=(j == 0), stop=False)
                    nc.tensor.matmul(ps_acc[t.odd], hi, sup_lo[:, j, :], start=False, stop=False)
                pe.wait_ge(alo_done, made(t))
                for j in range(T):
                    lo = at_lo[t.odd][:, j * P:(j + 1) * P]
                    mm = nc.tensor.matmul(ps_acc[t.odd], lo, sup_hi[:, j, :], start=False, stop=(j == T - 1))
                mm.then_inc(acc_done, 1)

            pe.wait_ge(ident_done, 1)
            def step(s):
                if s.within(-1, T - 1):
                    transpose_h(s + 1)
                if s.within(0, T):
                    times_w(s)

            over_tiles(pe, step, *S_STEPS)
            pe.wait_ge(slo_done, T)

            def step2(m):
                if m.within(0, T):
                    times_support(m)
                if m.fixed and m.n == T - 2:
                    pe.wait_ge(ones_done, 1)
                    pe.wait_ge(row_ones, 1)
                    nc.tensor.matmul(ps_flag, ones_of_row[:], ones[:], start=True, stop=True).then_inc(all_ones, 1)

            over_tiles(pe, step2, *M_STEPS)


def attention_layer(nc, mem, psum, adj, pairs, wq, bq, wk, bk, out):
    N, D = out.shape
    C = D // P
    T = -(-N // P)
    NP = T * P
    QUARTER = NP // QUADS
    SHORT = Q - (NP - N)
    DK = D // HEADS
    E = pairs.shape[0]
    EROWS = max(r for r in range(1, P + 1) if E % r == 0)
    ECOLS = E // EROWS
    GROUPS = [(b, min(BANK // P, T - b)) for b in range(0, T, BANK // P)]
    COLS = [(c, min(BANK, NP - c)) for c in range(0, NP, BANK)]
    assert N * N < 1 << 24
    assert DK == 64

    with ExitStack() as ctx:
        def sb(name, shape, dt):
            return ctx.enter_context(nc.sbuf_tensor(name, shape, dt))

        def sem(name):
            return ctx.enter_context(nc.semaphore(name))

        x1, ident, ones = mem["x1"], mem["ident"], mem["ones"]
        rstd, nmr = mem["rstd"], mem["nmr"]
        h2 = mem["sup"][:].rearrange("p (t d) -> p t d", d=D)
        kT = mem["work"][:].rearrange("p (c n) -> p c n", c=C)
        wkT = mem["weights"][:, 0:C * D].rearrange("p (c d) -> p c d", c=C)
        wqT = mem["adjT"][:, 0:C * D].rearrange("p (c d) -> p c d", c=C)
        w_rows = mem["rows_out"][:, 0, :]
        result = mem["rows_out"][:, 1, :]
        h2_tile = mem["h"][:, 0, :]
        x1_tile = mem["h"][:, 1, :]
        h2T = mem["hT"][:, 0:2 * D].bitcast(F32)
        qT = mem["hT"][:, 2 * D:4 * D].bitcast(F32)
        wide = [x1[:].rearrange("p t d -> p (t d)")[:, k * NP:(k + 1) * NP] for k in range(4)]
        bias_of, scale_of, score, factor = wide
        factor_blocks = factor.rearrange("p (b r j) -> p r b j", r=QUADS, j=Q)
        off_diag = mem["bias"][:, 0:P]
        diag = mem["bias"][:, P:2 * P]

        bqT = sb("bqT", [P, C], F32)
        bkT = sb("bkT", [P, C], F32)
        pair_ids = sb("pair_ids", [EROWS, ECOLS, 2], I32)
        places = sb("places", [EROWS, ECOLS], U32)
        place = sb("place", [EROWS, 1], U32)
        held = sb("held_scatter", [P, 1], F32)
        top = sb("top", [P, 1], F32)
        minus_top = sb("minus_top", [P, 1], F32)
        total = sb("total", [P, 1], F32)
        share = sb("share", [P, 1], F32)
        x1_dram = nc.dram_tensor("x1_tiles", [P, T * D], F32).ap()
        listed_dram = nc.dram_tensor("listed_pairs", [N * N, 1], F32).ap()
        listed_rows = listed_dram.rearrange("(r c) a -> r (c a)", c=N)

        ps_T, ps_P, ps_O = (psum[:, b, :] for b in (0, 1, 4))
        ps_S = [psum[:, 2 + k, :] for k in range(2)]

        small_in = sem("small_in")
        x1_saved = sem("x1_saved")
        w_rows_in = sem("w_rows_in")
        wT_done = sem("wT_done")
        wT_kept = sem("wT_kept")
        h2_made = sem("h2_made")
        h2_kept = sem("h2_kept")
        h2T_done = sem("h2T_done")
        h2T_kept = sem("h2T_kept")
        k_done = sem("k_done")
        k_kept = sem("k_kept")
        wide_clear = sem("wide_clear")
        zeros_stored = sem("zeros_stored")
        places_done = sem("places_done")
        place_done = sem("place_done")
        scattered = sem("scattered")
        diag_blank = sem("diag_blank")
        diag_done = sem("diag_done")
        tile_in = sem("tile_in")
        q_tile = sem("q_tile")
        qh_done = sem("qh_done")
        qh_kept = sem("qh_kept")
        q_done = sem("q_done")
        q_kept = sem("q_kept")
        chain = sem("chain")
        dots_done = sem("dots_done")
        dots_used = sem("dots_used")
        top_done = sem("top_done")
        exp_done = sem("exp_done")
        factor_done = sem("factor_done")
        meanT_done = sem("meanT_done")
        meanT_kept = sem("meanT_kept")
        product_done = sem("product_done")
        result_done = sem("result_done")
        result_stored = sem("result_stored")

        def dots(head, k):
            return ps_S[(head * len(COLS) + k) % 2]

        def of_tile(array, t):
            return array.rearrange("p (r c) -> p r c", r=QUADS)[:, :, bass.ds(t * Q, Q)]

        def quads(array):
            return array.rearrange("p (r i) -> p r i", r=QUADS)

        LOADS = 2 * QUADS + 1
        block = ctx.enter_context(nc.Block())

        @block.sync
        def _(sp):
            sp.dma_start(pair_ids[:], pairs.rearrange("(p c) k -> p c k", p=EROWS)).then_inc(small_in, 16)
            for k in range(C):
                sp.dma_start(bqT[:, k:k + 1], bq.rearrange("(c p a) -> c p a", p=P, a=1)[k]).then_inc(small_in, 16)
                sp.dma_start(bkT[:, k:k + 1], bk.rearrange("(c p a) -> c p a", p=P, a=1)[k]).then_inc(small_in, 16)
            sp.dma_start(x1_dram, x1[:].rearrange("p t d -> p (t d)")).then_inc(x1_saved, 16)
            for n in range(2 * C):
                w = wk if n < C else wq
                wait(sp, wT_done, n)
                sp.dma_start(w_rows, w[(n % C) * P:(n % C + 1) * P, :]).then_inc(w_rows_in, 16)

            sp.wait_ge(wide_clear, 1)
            with sp.Fori(0, T - 1) as t:
                sp.dma_start(listed_rows[bass.ds(t * P, P), :], score[:, 0:N]).then_inc(zeros_stored, 16)
            sp.dma_start(listed_rows[(T - 1) * P:N, :], score[0:N - (T - 1) * P, 0:N]).then_inc(zeros_stored, 16)
            sp.wait_ge(zeros_stored, 16 * T)
            sp.wait_ge(scattered, 16 * ECOLS)

            def tile(t, last):
                wait(sp, result_done, t)
                for q, a, b in quad_parts(last, SHORT):
                    at, to = bass.ds(q * QUARTER + t * Q + a, b - a), slice(q * Q + a, q * Q + b)
                    sp.dma_start(bias_of[to, 0:N], adj[at, :]).then_inc(tile_in, 16)
                    sp.dma_start(scale_of[to, 0:N], listed_rows[at, :]).then_inc(tile_in, 16)
                sp.dma_start(x1_tile, x1_dram[:, bass.ds(t * D, D)]).then_inc(tile_in, 16)
                sp.wait_ge(result_done, t + 1)
                for q, a, b in quad_parts(last, SHORT):
                    sp.dma_start(out[bass.ds(q * QUARTER + t * Q + a, b - a), :],
                                 result[q * Q + a:q * Q + b, :]).then_inc(result_stored, 16)

            tile(0, False)
            with sp.Fori(1, T - 1) as t:
                tile(t, False)
            tile(T - 1, True)
            sp.wait_ge(result_stored, 16 * (QUADS * (T - 1) + len(quad_parts(True, SHORT))))

        @block.gpsimd
        def _(pool):
            nc.gpsimd.memset(off_diag, 1.0)
            nc.gpsimd.memset(diag, 0.0).then_inc(diag_blank, 1)
            pool.wait_ge(diag_blank, 1)
            for block_, fill in ((off_diag, 0.0), (diag, SELF_SCORE)):
                ins = nc.gpsimd.affine_select(out=block_, in_=block_, compare_op=ALU.not_equal, fill=fill, base=0,
                                              pattern=[[-1, P]], channel_multiplier=1)
            ins.then_inc(diag_done, 1)

            pool.wait_ge(places_done, 1)
            pool.wait_ge(zeros_stored, 16 * T)

            def scatter(j):
                wait(pool, scattered, j * 16)
                nc.gpsimd.tensor_copy(place[:], places[:, bass.ds(j, 1)]).then_inc(place_done, 1)
                pool.wait_ge(place_done, j + 1)
                nc.gpsimd.tensor_tensor(held[:], ones[:], ones[:], ALU.mult)
                nc.gpsimd.indirect_dma_start(out=listed_dram, in_=ones[0:EROWS, :], in_offset=None,
                                             out_offset=bass.IndirectOffsetOnAxis(ap=place[:], axis=0)
                                             ).then_inc(scattered, 16)

            scatter(0)
            if ECOLS > 1:
                with pool.Fori(1, ECOLS) as j:
                    scatter(j)

        @block.scalar
        def _(act):
            def make_h2(t):
                wait(act, h2T_done, t)
                wait(act, h2_kept, t)
                nc.scalar.activation(h2_tile, x1[:, t, :], ACT.Relu, bias=nmr[:, bass.ds(t, 1)],
                                     scale=rstd[:, bass.ds(t, 1)]).then_inc(h2_made, 1)
                act.wait_ge(h2_made, t + 1)
                nc.scalar.activation(h2[:, t, :], h2_tile, ACT.Copy).then_inc(h2_kept, 1)

            make_h2(0)
            with act.Fori(1, T) as t:
                make_h2(t)

            def tile(t):
                act.wait_ge(qh_done, t)
                nc.scalar.activation(h2_tile, h2[:, t, :], ACT.Copy).then_inc(q_tile, 1)
                for head in range(HEADS):
                    act.wait_ge(top_done, t * HEADS + head + 1)
                    nc.scalar.activation(score[:, :], score[:, :], ACT.Exp, bias=minus_top[:], scale=1.0,
                                         accum_out=total[:]).then_inc(exp_done, 1)

            act.wait_ge(h2T_done, T)
            act.wait_ge(h2_kept, T)
            with act.Fori(0, T) as t:
                tile(t)

        @block.vector
        def _(dve):
            for n in range(2 * C):
                dve.wait_ge(wT_done, n + 1)
                wT, oc = (wkT, n) if n < C else (wqT, n - C)
                nc.vector.tensor_copy(wT[:, :, oc * P:(oc + 1) * P],
                                      ps_T.rearrange("p (c n) -> p c n", c=C)).then_inc(wT_kept, 1)
            dve.wait_ge(small_in, 16 * (1 + 2 * C))
            nc.vector.scalar_tensor_tensor(out=places[:], in0=pair_ids[:, :, 0], scalar=float(N),
                                           in1=pair_ids[:, :, 1], op0=ALU.mult, op1=ALU.add).then_inc(places_done, 1)

            def keep_k(t):
                dve.wait_ge(h2T_done, t + 1)
                wait(dve, k_done, t)
                nc.vector.tensor_copy(h2T, ps_T).then_inc(h2T_kept, 1)
                dve.wait_ge(k_done, t + 1)
                for c in range(C):
                    ins = nc.vector.tensor_scalar(of_tile(kT[:, c, :], t), quads(ps_P[:, c * P:(c + 1) * P]),
                                                  bkT[:, c:c + 1], None, ALU.add)
                ins.then_inc(k_kept, 1)

            keep_k(0)
            with dve.Fori(1, T) as t:
                keep_k(t)
            dve.wait_ge(x1_saved, 16)
            dve.wait_ge(h2_kept, T)
            nc.vector.memset(x1[:], 0.0).then_inc(wide_clear, 1)
            dve.wait_ge(zeros_stored, 16 * T)
            dve.wait_ge(diag_done, 1)

            LINKS = 5 + HEADS * 4

            def tile(t, loads):
                made = [0]

                def link(ins):
                    made[0] += 1
                    ins.then_inc(chain, 1)
                    dve.wait_ge(chain, t * LINKS + made[0])

                dve.wait_ge(qh_done, t + 1)
                wait(dve, q_done, t)
                nc.vector.tensor_copy(h2T, ps_T).then_inc(qh_kept, 1)
                dve.wait_ge(q_done, t + 1)
                wait(dve, dots_done, t * HEADS * len(COLS))
                for c in range(C):
                    ins = nc.vector.tensor_scalar(qT[:, c * P:(c + 1) * P], ps_P[:, c * P:(c + 1) * P],
                                                  bqT[:, c:c + 1], None, ALU.add)
                ins.then_inc(q_kept, 1)

                dve.wait_ge(tile_in, loads)
                link(nc.vector.tensor_scalar(bias_of, bias_of, 1.0, None, ALU.is_equal))
                link(nc.vector.scalar_tensor_tensor(out=scale_of, in0=scale_of, scalar=float(DK) ** -0.5,
                                                    in1=bias_of, op0=ALU.mult, op1=ALU.mult))
                link(nc.vector.tensor_scalar(bias_of, bias_of, -1.0, MASKED, ALU.add, ALU.mult))
                own_scale, own_bias = of_tile(scale_of, t), of_tile(bias_of, t)
                nc.vector.tensor_tensor(own_scale, own_scale, quads(off_diag), ALU.mult)
                link(nc.vector.tensor_tensor(own_bias, own_bias, quads(off_diag), ALU.mult))
                link(nc.vector.tensor_tensor(own_bias, own_bias, quads(diag), ALU.add))

                for head in range(HEADS):
                    for k, (c, n) in enumerate(COLS):
                        dve.wait_ge(dots_done, (t * HEADS + head) * len(COLS) + k + 1)
                        ins = nc.vector.tensor_tensor(score[:, c:c + n], dots(head, k)[:, 0:n], scale_of[:, c:c + n],
                                                      ALU.mult)
                        ins.then_inc(dots_used, 1)
                    dve.wait_ge(dots_used, (t * HEADS + head + 1) * len(COLS))
                    link(nc.vector.tensor_tensor(score, score, bias_of, ALU.add))
                    link(nc.vector.tensor_reduce(top[:], score, AX.X, ALU.max))
                    nc.vector.tensor_scalar(minus_top[:], top[:], -1.0, None, ALU.mult).then_inc(top_done, 1)
                    dve.wait_ge(exp_done, t * HEADS + head + 1)
                    link(nc.vector.reciprocal(share[:], total[:]))
                    link(nc.vector.tensor_scalar(share[:], share[:], 1.0 / HEADS, None, ALU.mult))
                    for r in range(QUADS):
                        prob, mean = score[:, r * QUARTER:(r + 1) * QUARTER], factor_blocks[:, r]
                        prob = prob.rearrange("p (b j) -> p b j", j=Q)
                        if head == 0:
                            ins = nc.vector.tensor_scalar(mean, prob, share[:], None, ALU.mult)
                        else:
                            ins = nc.vector.scalar_tensor_tensor(out=mean, in0=prob, scalar=share[:], in1=mean,
                                                                 op0=ALU.mult, op1=ALU.add)
                    ins.then_inc(factor_done, 1)
                    dve.wait_ge(factor_done, t * HEADS + head + 1)

                for g, (b, n) in enumerate(GROUPS):
                    dve.wait_ge(meanT_done, t * len(GROUPS) + g + 1)
                    nc.vector.tensor_copy(score[:, b * P:(b + n) * P], ps_T[:, 0:n * P]).then_inc(meanT_kept, 1)
                dve.wait_ge(product_done, t + 1)
                wait(dve, result_stored, t * 16 * QUADS)
                nc.vector.tensor_tensor(result, ps_O, x1_tile, ALU.add).then_inc(result_done, 1)

            tile(0, 16 * LOADS)
            with dve.Fori(1, T - 1) as t:
                tile(t, (t + 1) * 16 * LOADS)
            tile(T - 1, 16 * (LOADS * (T - 1) + 2 * len(quad_parts(True, SHORT)) + 1))

        @block.tensor
        def _(pe):
            for n in range(2 * C):
                pe.wait_ge(w_rows_in, 16 * (n + 1))
                wait(pe, wT_kept, n)
                for c in range(C):
                    mm = nc.tensor.transpose(ps_T[:, c * P:(c + 1) * P], w_rows[:, c * P:(c + 1) * P], ident[:])
                mm.then_inc(wT_done, 1)
            pe.wait_ge(wT_kept, 2 * C)

            def transpose_h2(done):
                for c in range(C):
                    mm = nc.tensor.transpose(ps_T[:, c * P:(c + 1) * P], h2_tile[:, c * P:(c + 1) * P], ident[:])
                mm.then_inc(done, 1)

            def project(wT, done):
                for c in range(C):
                    for k in range(C):
                        mm = nc.tensor.matmul(ps_P[:, c * P:(c + 1) * P], wT[:, k, c * P:(c + 1) * P],
                                              h2T[:, k * P:(k + 1) * P], start=(k == 0), stop=(k == C - 1))
                mm.then_inc(done, 1)

            def keys(t):
                pe.wait_ge(h2_made, t + 1)
                wait(pe, h2T_kept, t)
                transpose_h2(h2T_done)
                pe.wait_ge(h2T_kept, t + 1)
                wait(pe, k_kept, t)
                project(wkT, k_done)

            keys(0)
            with pe.Fori(1, T) as t:
                keys(t)
            pe.wait_ge(k_kept, T)
            pe.wait_ge(h2_kept, T)

            def tile(t):
                pe.wait_ge(q_tile, t + 1)
                wait(pe, qh_kept, t)
                transpose_h2(qh_done)
                pe.wait_ge(qh_kept, t + 1)
                wait(pe, q_kept, t)
                project(wqT, q_done)
                pe.wait_ge(q_kept, t + 1)
                for head in range(HEADS):
                    c, lanes = head * DK // P, slice(head * DK % P, head * DK % P + DK)
                    for k, (col, n) in enumerate(COLS):
                        wait(pe, dots_used, (t * HEADS + head) * len(COLS) + k - 1)
                        nc.tensor.matmul(dots(head, k)[:, 0:n], qT[lanes, c * P:(c + 1) * P],
                                         kT[lanes, c, col:col + n], start=True, stop=True).then_inc(dots_done, 1)
                pe.wait_ge(factor_done, (t + 1) * HEADS)
                for g, (b, n) in enumerate(GROUPS):
                    wait(pe, meanT_kept, t * len(GROUPS) + g)
                    for j in range(n):
                        mm = nc.tensor.transpose(ps_T[:, j * P:(j + 1) * P], factor[:, (b + j) * P:(b + j + 1) * P],
                                                 ident[:])
                    mm.then_inc(meanT_done, 1)
                pe.wait_ge(meanT_kept, (t + 1) * len(GROUPS))
                wait(pe, result_done, t)
                for j in range(T):
                    mm = nc.tensor.matmul(ps_O, score[:, j * P:(j + 1) * P], h2[:, j, :], start=(j == 0),
                                          stop=(j == T - 1))
                mm.then_inc(product_done, 1)

            tile(0)
            with pe.Fori(1, T) as t:
                tile(t)


_INS = ['x', 'adj', 'L0_gnn_weight', 'L0_gnn_bias', 'L1_gnn_rel_pair_index', 'L1_gnn_Wq', 'L1_gnn_bq',
        'L1_gnn_Wk', 'L1_gnn_bk']


def kernel(**inputs):
    import numpy as _np
    import concourse.bacc as _bacc
    from concourse import mybir as _mybir
    from concourse.bass_utils import run_bass_kernel_spmd as _run

    nc = _bacc.Bacc("TRN2", target_bir_lowering=False, num_devices=1)
    arrays, args = {}, []
    for name in _INS:
        a = _np.ascontiguousarray(inputs[name])
        arrays[f"in_{name}_dram"] = a
        args.append(nc.dram_tensor(f"in_{name}_dram", a.shape, _mybir.dt.from_np(a.dtype), kind="ExternalInput").ap())
    args.append(nc.dram_tensor("out_0_dram", inputs['x'].shape, _mybir.dt.float32, kind="ExternalOutput").ap())
    gnn_kernel(nc, *args)
    r = _run(nc, [arrays], core_ids=[0])
    return r.results[0]["out_0_dram"]
```

```python
from contextlib import ExitStack

import concourse.bass as bass
from concourse import mybir

P = 128
Q = 32
QUADS = P // Q
BANK = 512
ALU = mybir.AluOpType
ACT = mybir.ActivationFunctionType
AX = mybir.AxisListType
F32 = mybir.dt.float32
F16 = mybir.dt.float16
BF16 = mybir.dt.bfloat16
I32 = mybir.dt.int32
U32 = mybir.dt.uint32

HEADS = 8
EPS = 1e-5
MASKED = 1e30
SELF_SCORE = 1e-7

W_SCALE = 64.0
H_SCALE = 8.0
ADJ_SCALE = 256.0
SUP_SCALE = 64.0


class Tile:

    def __init__(self, half, odd):
        self.half, self.odd = half, odd
        self.n = half * 2 + odd
        self.fixed = isinstance(half, int)

    def __add__(self, k):
        return Tile(self.half + (self.odd + k) // 2, (self.odd + k) % 2)

    def within(self, a, b):
        return not self.fixed or a <= self.n < b


def fixed(n):
    return Tile(n // 2, n % 2)


def over_tiles(eng, step, first, loop, tail, end):
    for n in range(first, loop):
        step(fixed(n))
    if tail > loop:
        with eng.Fori(loop // 2, tail // 2) as i:
            step(Tile(i, 0))
            step(Tile(i, 1))
    for n in range(tail, end):
        step(fixed(n))


def wait(eng, sem, count):
    if not isinstance(count, int) or count > 0:
        eng.wait_ge(sem, count)


def row_parts(rows):
    full = rows - rows % 16
    return [(a, b) for a, b in ((0, full), (full, rows)) if b > a]


def quad_parts(last, short):
    return [(q, a, b) for q in range(QUADS) for a, b in (row_parts(short) if last and q == QUADS - 1 else [(0, Q)])]


def dram_view(tensor, row, col, steps, cols):
    width = tensor.shape[1]
    return bass.AP(tensor.tensor, row * width + col, [[r * width, n] for r, n in steps] + [[1, cols]])




def gnn_kernel(nc, x, adj, w0, b0, pairs, wq, bq, wk, bk, out):
    N, D = x.shape
    T = -(-N // P)
    NP = T * P
    assert D == BANK and T % 2 == 0 and T >= 16 and 0 < NP - N < Q

    with ExitStack() as ctx:
        def sb(name, shape, dt):
            return ctx.enter_context(nc.sbuf_tensor(name, shape, dt))

        mem = {
            "x1": sb("x1", [P, T, D], F32),
            "sup": sb("sup", [P, T * D], F32),
            "work": sb("work", [P, 4 * NP], F32),
            "ident": sb("ident", [P, P], F32),
            "ones": sb("ones", [P, 1], F32),
            "rstd": sb("rstd", [P, T], F32),
            "nmr": sb("nmr", [P, T], F32),
            "adjT": sb("adjT", [P, NP], F32),
            "weights": sb("weights", [P, 4 * D], F32),
            "rows_out": sb("rows_out", [P, 2, D], F32),
            "h": sb("h", [P, 2, D], F32),
            "hT": sb("hT", [P, 4 * D], F16),
            "bias": sb("bias", [P, D], F32),
            "flag": sb("flag", [1, 1], I32),
        }
        psum = ctx.enter_context(nc.psum_tensor("psum", [P, 8, BANK], F32))
        layer0_and_diagonal(nc, mem, psum, x, adj, w0, b0, out)
        ones_found = nc.values_load(mem["flag"][0:1, 0:1], min_val=0, max_val=P * NP)
        with nc.If(ones_found > 0):
            attention_layer(nc, mem, psum, adj, pairs, wq, bq, wk, bk, out)


def layer0_and_diagonal(nc, mem, psum, x, adj, w0, b0, out):
    N, D = x.shape
    C = D // P
    T = -(-N // P)
    NP = T * P
    QUARTER = NP // QUADS
    SHORT = Q - (NP - N)
    HALVES = 2
    WARM_UP = 20
    CHUNKS = 4
    CUTS = [k * T // CHUNKS for k in range(CHUNKS + 1)]
    S_STEPS = (0, 2, T - 8, T + 1)
    M_STEPS = (-1, 2, T - 4, T)

    with ExitStack() as ctx:
        def sb(name, shape, dt):
            return ctx.enter_context(nc.sbuf_tensor(name, shape, dt))

        def sem(name):
            return ctx.enter_context(nc.semaphore(name))

        x1, ident, ones, bias = mem["x1"], mem["ident"], mem["ones"], mem["bias"]
        rstd, nmr, rows_out, h, flag = mem["rstd"], mem["nmr"], mem["rows_out"], mem["h"], mem["flag"]
        sup = [mem["sup"][:, k * T * D // 2:(k + 1) * T * D // 2].bitcast(F16)
               .rearrange("p (t d) -> p t d", d=D) for k in range(2)]
        sup_hi, sup_lo = sup
        work = mem["work"]
        adj_raw = [work[:, k * NP:(k + 1) * NP] for k in range(2)]
        at = [work[:, (2 + k) * NP:(3 + k) * NP].bitcast(F16) for k in range(2)]
        at_hi = [a[:, 0:NP] for a in at]
        at_lo = [a[:, NP:2 * NP] for a in at]
        adjT = mem["adjT"]
        w_raw = work[:, 3 * NP:3 * NP + C * D].rearrange("p (c d) -> p c d", c=C)
        w_halves = mem["weights"][:].bitcast(F16)
        w_hi = w_halves[:, 0:C * D].rearrange("p (c d) -> p c d", c=C)
        w_lo = w_halves[:, C * D:2 * C * D].rearrange("p (c d) -> p c d", c=C)
        hT_hi = mem["hT"][:, 0:2 * D].rearrange("p (k d) -> p k d", k=2)
        hT_lo = mem["hT"][:, 2 * D:4 * D].rearrange("p (k d) -> p k d", k=2)
        bn6 = sb("bn6", [P, 2, 6], F32)
        mv = sb("mv", [P, 2, 2], F32)
        ve = sb("ve", [P, 2], F32)
        sd = sb("sd", [P, 2], F32)
        r0 = sb("r0", [P, 2], F32)
        r1 = sb("r1", [P, 2], F32)
        minus_one = sb("minus_one", [P, 2], F32)
        three_halves = sb("three_halves", [P, 2], F32)
        minus_mean = sb("minus_mean", [P, 2], F32)
        eps = sb("eps", [P, 1], F32)
        ones_seen = sb("ones_seen", [P, T * HALVES], F32)
        held = sb("held", [P, 2], F32)
        ones_of_row = sb("ones_of_row", [P, 1], F32)
        ps_hT, ps_sup, ps_acc = ([psum[:, b + k, :] for k in range(2)] for b in (0, 2, 4))
        ps_flag = psum[0:1, 6, 0:1]
        is_one = psum[:, 0:4, :].rearrange("p b n -> p (b n)")[:, 0:NP // HALVES]

        x_in = [sem(f"x_in{k}") for k in range(2)]
        adj_in = [sem(f"adj_in{k}") for k in range(2)]
        stored = [sem(f"stored{k}") for k in range(2)]
        w_in = [sem(f"w_in{c}") for c in range(C)]
        bias_in = sem("bias_in")
        padded = sem("padded")
        blank = sem("blank")
        ident_done = sem("ident_done")
        ones_done = sem("ones_done")
        zeros_done = sem("zeros_done")
        w_hi_done = sem("w_hi_done")
        w_lo_done = sem("w_lo_done")
        linked = sem("linked")
        pool_linked = sem("pool_linked")
        ve_done = sem("ve_done")
        recip_done = sem("recip_done")
        var_done = sem("var_done")
        root_done = sem("root_done")
        stat_done = sem("stat_done")
        h_done = sem("h_done")
        hT_done = sem("hT_done")
        hhi_done = sem("hhi_done")
        hlo_done = sem("hlo_done")
        sup_done = sem("sup_done")
        shi_done = sem("shi_done")
        slo_done = sem("slo_done")
        bias_added = sem("bias_added")
        adjT_done = sem("adjT_done")
        ahi_done = sem("ahi_done")
        alo_done = sem("alo_done")
        counted = sem("counted")
        acc_done = sem("acc_done")
        x1_done = sem("x1_done")
        h2_done = sem("h2_done")
        rows_done = sem("rows_done")
        row_ones = sem("row_ones")
        all_ones = sem("all_ones")
        flag_done = sem("flag_done")

        block = ctx.enter_context(nc.Block())

        def last(t):
            return t.fixed and t.n == T - 1

        def adj_parts(t):
            if not last(t):
                return [(q, 0, QUADS, 0, Q) for q in range(QUADS)]
            return [(q, first, n, a, b) for q in range(QUADS)
                    for first, n, a, b in [(0, QUADS - 1, 0, Q)] + [(QUADS - 1, 1, a, b) for a, b in row_parts(SHORT)]]

        def made(t):
            return t.n + CHUNKS

        def adj_landed(t):
            return 16 * (t.half * len(adj_parts(fixed(0))) + len(adj_parts(t)))

        @block.sync
        def _(sp):
            def load_x(t):
                wait(sp, x_in[t.odd], t.half * 16)
                whole = QUADS - last(t)
                if last(t):
                    sp.wait_ge(padded, 1)
                sp.dma_start(x1[0:whole * Q, t.n, :],
                             dram_view(x, t.n * Q, 0, [(QUARTER, whole), (1, Q)], D)).then_inc(x_in[t.odd], 16)
                if last(t):
                    first = whole * QUARTER + t.n * Q
                    for a, b in row_parts(SHORT):
                        sp.dma_start(x1[whole * Q + a:whole * Q + b, t.n, :],
                                     x[first + a:first + b, :]).then_inc(x_in[t.odd], 16)

            def load_w(chunks):
                for c in chunks:
                    sp.dma_start(w_raw[:, c, :], w0[c * P:(c + 1) * P, :]).then_inc(w_in[c], 16)

            load_x(fixed(0))
            load_x(fixed(1))
            load_w(range(0, C // 2))
            load_x(fixed(2))
            load_x(fixed(3))
            load_w(range(C // 2, C))
            sp.dma_start(bias[:], b0.rearrange("(a d) -> a d", a=1).broadcast_to([P, D])).then_inc(bias_in, 16)
            over_tiles(sp, load_x, 4, 4, T - 2, T)

            def load_adj(t):
                for q, first, n, a, b in adj_parts(t):
                    cols = QUARTER if q < QUADS - 1 else N - q * QUARTER
                    dst = adj_raw[t.odd].rearrange("p (r c) -> p r c", r=QUADS)[q * Q + a:q * Q + b,
                                                                                 first:first + n, 0:cols]
                    src = dram_view(adj, first * QUARTER + t.n * Q + a, q * QUARTER, [(1, b - a), (QUARTER, n)], cols)
                    sp.dma_start(dst, src).then_inc(adj_in[t.odd], 16)

            def store(t):
                sp.wait_ge(rows_done, t.n + 1)
                whole = QUADS - last(t)
                sp.dma_start(dram_view(out, t.n * Q, 0, [(QUARTER, whole), (1, Q)], D),
                             rows_out[0:whole * Q, t.odd, :]).then_inc(stored[t.odd], 16)
                if last(t):
                    for a, b in row_parts(SHORT):
                        first = whole * QUARTER + t.n * Q
                        sp.dma_start(out[first + a:first + b, :],
                                     rows_out[whole * Q + a:whole * Q + b, t.odd, :]).then_inc(stored[t.odd], 16)

            sp.wait_ge(padded, 1)
            load_adj(fixed(0))
            load_adj(fixed(1))

            def step(m):
                if m.within(-1, T - 3):
                    sp.wait_ge(counted, (m.n + 2) * HALVES)
                    load_adj(m + 3)
                if m.within(1, T):
                    store(m + -1)

            over_tiles(sp, step, *M_STEPS)
            store(fixed(T - 1))
            sp.wait_ge(stored[0], 16 * (T // 2))
            sp.wait_ge(stored[1], 16 * (T // 2 + len(row_parts(SHORT))))

        @block.gpsimd
        def _(pool):
            nc.gpsimd.memset(minus_one[:], -1.0)
            nc.gpsimd.memset(three_halves[:], 1.5)
            nc.gpsimd.memset(ident[:], 0.0).then_inc(blank, 1)
            pool.wait_ge(blank, 1)
            nc.gpsimd.affine_select(out=ident[:], in_=ident[:], compare_op=ALU.not_equal, fill=1.0, base=0,
                                    pattern=[[-1, P]], channel_multiplier=1).then_inc(ident_done, 1)

            def add_bias(t):
                pool.wait_ge(h_done, t.n + 1)
                nc.gpsimd.tensor_tensor(x1[:, t.n, :], x1[:, t.n, :], bias[:], ALU.add).then_inc(bias_added, 1)

            def add_rows(t):
                pool.wait_ge(h2_done, t.n + 1)
                nc.gpsimd.tensor_tensor(rows_out[:, t.odd, :], rows_out[:, t.odd, :], x1[:, t.n, :],
                                        ALU.add).then_inc(rows_done, 1)

            LINKS = 4

            def scales(t):
                made = [0]

                def link(ins):
                    made[0] += 1
                    ins.then_inc(pool_linked, 1)
                    pool.wait_ge(pool_linked, t.half * LINKS + made[0])

                pool.wait_ge(recip_done, t.half + 1)
                pool.wait_ge(ve_done, t.half + 1)
                pair = bass.ds(t.n, 2)
                nc.gpsimd.tensor_tensor(minus_mean[:], mv[:, :, 0], minus_one[:], ALU.mult)
                link(nc.gpsimd.tensor_tensor(r1[:], r0[:], r0[:], ALU.mult))
                link(nc.gpsimd.tensor_tensor(r1[:], r1[:], ve[:], ALU.mult))
                link(nc.gpsimd.tensor_tensor(r1[:], r1[:], three_halves[:], ALU.add))
                link(nc.gpsimd.tensor_tensor(rstd[:, pair], r0[:], r1[:], ALU.mult))
                nc.gpsimd.tensor_tensor(nmr[:, pair], minus_mean[:], rstd[:, pair], ALU.mult).then_inc(stat_done, 1)

            def step(s):
                if s.odd == 0 and s.within(0, T - 4):
                    scales(s + 4)
                if s.within(0, T - 3):
                    add_bias(s + 3)

            scales(fixed(0))
            scales(fixed(2))
            pool.wait_ge(bias_in, 16)
            for n in range(3):
                add_bias(fixed(n))
            over_tiles(pool, step, *S_STEPS)
            over_tiles(pool, add_rows, 0, 0, T - 2, T - 1)

        @block.scalar
        def _(act):
            def root(n, count):
                act.wait_ge(var_done, count)
                nc.scalar.activation(sd[:, 0:n], mv[:, 0:n, 1], ACT.Sqrt, bias=eps[:]).then_inc(root_done, 1)

            def normalize(t):
                act.wait_ge(stat_done, t.half + 1)
                wait(act, hT_done, t.n - 1)
                nc.scalar.activation(h[:, t.odd, :], x1[:, t.n, :], ACT.Relu, bias=nmr[:, bass.ds(t.n, 1)],
                                     scale=rstd[:, bass.ds(t.n, 1)]).then_inc(h_done, 1)

            def h_high(t):
                act.wait_ge(hT_done, t.n + 1)
                wait(act, sup_done, t.n - 1)
                nc.scalar.activation(hT_hi[:, t.odd, :], ps_hT[t.odd], ACT.Copy,
                                     scale=H_SCALE).then_inc(hhi_done, 1)

            def sup_high(t):
                act.wait_ge(sup_done, t.n + 1)
                nc.scalar.activation(sup_hi[:, t.n, :], ps_sup[t.odd], ACT.Copy,
                                     scale=SUP_SCALE / (W_SCALE * H_SCALE)).then_inc(shi_done, 1)

            def adj_high(t):
                act.wait_ge(adjT_done, made(t))
                wait(act, acc_done, t.n - 1)
                nc.scalar.activation(at_hi[t.odd], adjT[:], ACT.Copy, scale=ADJ_SCALE).then_inc(ahi_done, 1)

            def adj_high_chunk(k):
                cols = slice(CUTS[k] * P, CUTS[k + 1] * P)
                act.wait_ge(adjT_done, k + 1)
                nc.scalar.activation(at_hi[0][:, cols], adjT[:, cols], ACT.Copy, scale=ADJ_SCALE).then_inc(ahi_done, 1)

            def step(s):
                if s.within(1, T - 1):
                    h_high(s + 1)
                if s.odd == 0 and s.within(0, T - 4):
                    root(2, s.half + 3)
                if s.within(1, T + 1):
                    sup_high(s + -1)
                if s.within(0, T - 3):
                    normalize(s + 3)
                if s.fixed and s.n > T - 4:
                    adj_high_chunk(s.n - (T - 4) - 1)

            def w_high(c):
                act.wait_ge(w_in[c], 16)
                nc.scalar.activation(w_hi[:, c, :], w_raw[:, c, :], ACT.Copy, scale=W_SCALE).then_inc(w_hi_done, 1)

            root(2, 1)
            for c in range(C // 2):
                w_high(c)
            normalize(fixed(0))
            normalize(fixed(1))
            h_high(fixed(0))
            root(2, 2)
            for c in range(C // 2, C):
                w_high(c)
            h_high(fixed(1))
            normalize(fixed(2))
            over_tiles(act, step, *S_STEPS)

            def normalize_x1(t):
                act.wait_ge(stat_done, T // 2 + t.n + 1)
                wait(act, stored[t.odd], t.half * 16)
                nc.scalar.activation(rows_out[:, t.odd, :], x1[:, t.n, :], ACT.Relu,
                                     bias=nmr[:, bass.ds(t.n, 1)],
                                     scale=rstd[:, bass.ds(t.n, 1)]).then_inc(h2_done, 1)

            def step2(m):
                if m.within(0, T - 1):
                    adj_high(m + 1)
                if m.within(1, T):
                    root(1, (m + -1).n + T // 2 + 1)
                    normalize_x1(m + -1)

            over_tiles(act, step2, *M_STEPS)
            root(1, T + T // 2)
            normalize_x1(fixed(T - 1))

        @block.vector
        def _(dve):
            def link(ins, count):
                ins.then_inc(linked, 1)
                dve.wait_ge(linked, count)

            def hold(k=0):
                nc.vector.memset(held[:, k:k + 1], 0.0)

            def variances(ins, n, link_count, count):
                link(ins, link_count)
                wait(dve, stat_done, count - 1)
                hold()
                for k in range(n):
                    ins = nc.vector.bn_aggr(mv[:, k, :], bn6[:, k, :])
                ins.then_inc(var_done, 1)
                dve.wait_ge(var_done, count)
                nc.vector.tensor_scalar(ve[:, 0:n], mv[:, 0:n, 1], EPS, -0.5, ALU.add, ALU.mult).then_inc(ve_done, 1)

            def reciprocals(n, count):
                dve.wait_ge(root_done, count)
                nc.vector.reciprocal(r0[:, 0:n], sd[:, 0:n]).then_inc(recip_done, 1)

            LINKS = 3

            nc.vector.memset(hT_hi[:, 0, :], 0.0).then_inc(zeros_done, 1)
            nc.vector.memset(eps[:], EPS)
            nc.vector.memset(x1[P - Q:P, T - 1, :], 0.0)
            for k in range(2):
                padding = adj_raw[k].rearrange("p (r c) -> p r c", r=QUADS)[P - Q:P, :, QUARTER - (NP - N):QUARTER]
                ins = nc.vector.memset(padding, 0.0)
            ins.then_inc(padded, 1)
            nc.vector.memset(ones[:], 1.0).then_inc(ones_done, 1)

            def h_low(t):
                dve.wait_ge(hhi_done, t.n + 1)
                nc.vector.scalar_tensor_tensor(out=hT_lo[:, t.odd, :], in0=ps_hT[t.odd], scalar=H_SCALE,
                                               in1=hT_hi[:, t.odd, :], op0=ALU.mult,
                                               op1=ALU.subtract).then_inc(hlo_done, 1)

            def sup_low(t):
                dve.wait_ge(shi_done, t.n + 1)
                nc.vector.scalar_tensor_tensor(out=sup_lo[:, t.n, :], in0=ps_sup[t.odd],
                                               scalar=SUP_SCALE / (W_SCALE * H_SCALE), in1=sup_hi[:, t.n, :],
                                               op0=ALU.mult, op1=ALU.subtract).then_inc(slo_done, 1)

            def transpose_adj(t, lo, hi):
                src = adj_raw[t.odd].rearrange("p (r b j) -> p r b j", r=QUADS, j=Q)
                dst = adjT[:].rearrange("p (b r i) -> p r b i", r=QUADS, i=Q)
                nc.vector.transpose(dst[:, :, lo:hi, :], src[:, :, lo:hi, :]).then_inc(adjT_done, 1)

            def adj_low(t):
                dve.wait_ge(ahi_done, made(t))
                nc.vector.scalar_tensor_tensor(out=at_lo[t.odd], in0=adjT[:], scalar=ADJ_SCALE, in1=at_hi[t.odd],
                                               op0=ALU.mult, op1=ALU.subtract).then_inc(alo_done, 1)

            def adj_low_chunk(k):
                cols = slice(CUTS[k] * P, CUTS[k + 1] * P)
                dve.wait_ge(ahi_done, k + 1)
                nc.vector.scalar_tensor_tensor(out=at_lo[0][:, cols], in0=adjT[:, cols], scalar=ADJ_SCALE,
                                               in1=at_hi[0][:, cols], op0=ALU.mult,
                                               op1=ALU.subtract).then_inc(alo_done, 1)

            def count_ones(t):
                for k in range(HALVES):
                    wait(dve, counted, t.n * HALVES + k)
                    nc.vector.tensor_scalar(is_one, adj_raw[t.odd][:, k * NP // 2:(k + 1) * NP // 2], 1.0, 0.0,
                                            ALU.is_equal, ALU.add,
                                            accum_out=ones_seen[:, bass.ds(t.n * HALVES + k, 1)]
                                            ).then_inc(counted, 1)

            def w_low(c):
                dve.wait_ge(w_hi_done, c + 1)
                nc.vector.scalar_tensor_tensor(out=w_lo[:, c, :], in0=w_raw[:, c, :], scalar=W_SCALE,
                                               in1=w_hi[:, c, :], op0=ALU.mult,
                                               op1=ALU.subtract).then_inc(w_lo_done, 1)

            def x_spread(t):
                dve.wait_ge(x_in[t.odd], 16 * (t.half + 1 + last(t) * len(row_parts(SHORT))))
                hold(t.odd)
                ins = nc.vector.bn_stats(bn6[:, t.odd, :], x1[:, t.n, :])
                if t.odd == 1:
                    variances(ins, 2, t.half + 1, t.half + 1)

            def step(s):
                if s.within(1, T - 1):
                    h_low(s + 1)
                if s.within(1, T + 1):
                    sup_low(s + -1)
                if s.within(0, T - 6):
                    x_spread(s + 6)
                if s.odd == 0 and s.within(0, T - 4):
                    reciprocals(2, s.half + 3)
                if s.fixed and s.n > T - 3:
                    adj_low_chunk(s.n - (T - 3) - 1)
                if s.fixed and T - 4 <= s.n < T:
                    k = s.n - (T - 4)
                    if k == 0:
                        dve.wait_ge(adj_in[0], adj_landed(fixed(0)))
                    transpose_adj(fixed(0), CUTS[k], CUTS[k + 1])

            x_spread(fixed(0))
            x_spread(fixed(1))
            reciprocals(2, 1)
            w_low(0)
            w_low(1)
            x_spread(fixed(2))
            x_spread(fixed(3))
            h_low(fixed(0))
            reciprocals(2, 2)
            for c in range(2, C):
                w_low(c)
            h_low(fixed(1))
            x_spread(fixed(4))
            x_spread(fixed(5))
            over_tiles(dve, step, *S_STEPS)

            def links_before(t):
                return t.n * LINKS + T // 2

            def scales(t):
                base = links_before(t) + 1
                reciprocals(1, t.n + T // 2 + 1)
                dve.wait_ge(recip_done, t.n + T // 2 + 1)
                dve.wait_ge(ve_done, t.n + T // 2 + 1)
                root, scale = r0[:, 0:1], rstd[:, bass.ds(t.n, 1)]
                link(nc.vector.scalar_tensor_tensor(out=r1[:, 0:1], in0=root, scalar=ve[:, 0:1], in1=root,
                                                    op0=ALU.mult, op1=ALU.mult), base + 1)
                link(nc.vector.scalar_tensor_tensor(out=scale, in0=r1[:, 0:1], scalar=1.5, in1=root,
                                                    op0=ALU.add, op1=ALU.mult), base + 2)
                nc.vector.scalar_tensor_tensor(out=nmr[:, bass.ds(t.n, 1)], in0=mv[:, 0:1, 0], scalar=-1.0,
                                               in1=scale, op0=ALU.mult, op1=ALU.mult).then_inc(stat_done, 1)

            def finish(t):
                dve.wait_ge(acc_done, t.n + 1)
                nc.vector.scalar_tensor_tensor(out=x1[:, t.n, :], in0=ps_acc[t.odd],
                                               scalar=1.0 / (ADJ_SCALE * SUP_SCALE), in1=x1[:, t.n, :],
                                               op0=ALU.mult, op1=ALU.add).then_inc(x1_done, 1)
                dve.wait_ge(x1_done, t.n + 1)
                hold()
                ins = nc.vector.bn_stats(bn6[:, 0, :], x1[:, t.n, :])
                variances(ins, 1, links_before(t) + 1, t.n + T // 2 + 1)

            adj_low_chunk(CHUNKS - 1)
            dve.wait_ge(bias_added, T)
            dve.wait_ge(slo_done, T)

            def step2(m):
                if m.within(1, T):
                    finish(m + -1)
                if m.within(0, T - 1):
                    adj_low(m + 1)
                if m.within(1, T):
                    scales(m + -1)
                if m.within(-1, T - 2):
                    t = m + 2
                    dve.wait_ge(adj_in[t.odd], adj_landed(t))
                    dve.wait_ge(alo_done, made(t + -1))
                    transpose_adj(t, 0, T)
                    if m.fixed and m.n == -1:
                        count_ones(fixed(0))
                    count_ones(t)
                if m.fixed and m.n == T - 2:
                    dve.wait_ge(counted, T * HALVES)
                    nc.vector.tensor_reduce(ones_of_row[:], ones_seen[:], AX.X, ALU.add).then_inc(row_ones, 1)
                if m.fixed and m.n == T - 1:
                    dve.wait_ge(all_ones, 1)
                    nc.vector.tensor_copy(flag[0:1, 0:1], ps_flag).then_inc(flag_done, 1)

            over_tiles(dve, step2, *M_STEPS)
            t = fixed(T - 1)
            finish(t)
            scales(t)
            dve.wait_ge(h2_done, T)
            dve.wait_ge(rows_done, T - 1)
            nc.vector.tensor_tensor(rows_out[:, t.odd, :], rows_out[:, t.odd, :], x1[:, t.n, :],
                                    ALU.add).then_inc(rows_done, 1)

        @block.tensor
        def _(pe):
            def transpose_h(t):
                pe.wait_ge(h_done, t.n + 1)
                wait(pe, hlo_done, t.n - 1)
                for c in range(C):
                    mm = nc.tensor.transpose(ps_hT[t.odd][:, c * P:(c + 1) * P], h[:, t.odd, c * P:(c + 1) * P],
                                             ident[:])
                mm.then_inc(hT_done, 1)

            def times_w(t):
                pe.wait_ge(hhi_done, t.n + 1)
                wait(pe, slo_done, t.n - 1)
                hi, lo = hT_hi[:, t.odd, :], hT_lo[:, t.odd, :]
                for c in range(C):
                    part = hi[:, c * P:(c + 1) * P]
                    if t.fixed and t.n == 0:
                        pe.wait_ge(w_lo_done, c + 1)
                    nc.tensor.matmul(ps_sup[t.odd], part, w_hi[:, c, :], start=(c == 0), stop=False)
                    nc.tensor.matmul(ps_sup[t.odd], part, w_lo[:, c, :], start=False, stop=False)
                pe.wait_ge(hlo_done, t.n + 1)
                for c in range(C):
                    mm = nc.tensor.matmul(ps_sup[t.odd], lo[:, c * P:(c + 1) * P], w_hi[:, c, :], start=False,
                                          stop=(c == C - 1))
                mm.then_inc(sup_done, 1)

            def times_support(t):
                wait(pe, x1_done, t.n - 1)
                first = t.fixed and t.n == 0
                if not first:
                    pe.wait_ge(ahi_done, made(t))
                for j in range(T):
                    if first and j in CUTS:
                        pe.wait_ge(ahi_done, CUTS.index(j) + 1)
                    if first and j >= T - 2:
                        pe.wait_ge(slo_done, j + 1)
                    hi = at_hi[t.odd][:, j * P:(j + 1) * P]
                    nc.tensor.matmul(ps_acc[t.odd], hi, sup_hi[:, j, :], start=(j == 0), stop=False)
                    nc.tensor.matmul(ps_acc[t.odd], hi, sup_lo[:, j, :], start=False, stop=False)
                if not first:
                    pe.wait_ge(alo_done, made(t))
                for j in range(T):
                    if first and j in CUTS:
                        pe.wait_ge(alo_done, CUTS.index(j) + 1)
                    lo = at_lo[t.odd][:, j * P:(j + 1) * P]
                    mm = nc.tensor.matmul(ps_acc[t.odd], lo, sup_hi[:, j, :], start=False, stop=(j == T - 1))
                mm.then_inc(acc_done, 1)

            def step(s):
                if s.within(0, T - 1):
                    transpose_h(s + 1)
                if s.within(0, T):
                    times_w(s)

            pe.wait_ge(zeros_done, 1)
            with pe.Fori(0, WARM_UP // 4):
                for _ in range(4):
                    nc.tensor.matmul(ps_acc[0], hT_hi[:, 0, 0:P], hT_hi[:, 0, :], start=True, stop=True)
            pe.wait_ge(ident_done, 1)
            transpose_h(fixed(0))
            over_tiles(pe, step, *S_STEPS)

            def step2(m):
                if m.within(0, T):
                    times_support(m)
                if m.fixed and m.n == T - 2:
                    pe.wait_ge(ones_done, 1)
                    pe.wait_ge(row_ones, 1)
                    nc.tensor.matmul(ps_flag, ones_of_row[:], ones[:], start=True, stop=True).then_inc(all_ones, 1)

            over_tiles(pe, step2, *M_STEPS)


def attention_layer(nc, mem, psum, adj, pairs, wq, bq, wk, bk, out):
    N, D = out.shape
    C = D // P
    T = -(-N // P)
    NP = T * P
    QUARTER = NP // QUADS
    SHORT = Q - (NP - N)
    DK = D // HEADS
    E = pairs.shape[0]
    EROWS = max(r for r in range(1, P + 1) if E % r == 0)
    ECOLS = E // EROWS
    GROUPS = [(b, min(BANK // P, T - b)) for b in range(0, T, BANK // P)]
    COLS = [(c, min(BANK, NP - c)) for c in range(0, NP, BANK)]
    assert N * N < 1 << 24
    assert DK == 64

    with ExitStack() as ctx:
        def sb(name, shape, dt):
            return ctx.enter_context(nc.sbuf_tensor(name, shape, dt))

        def sem(name):
            return ctx.enter_context(nc.semaphore(name))

        x1, ident, ones = mem["x1"], mem["ident"], mem["ones"]
        rstd, nmr = mem["rstd"], mem["nmr"]
        h2 = mem["sup"][:].rearrange("p (t d) -> p t d", d=D)
        kT = mem["work"][:].rearrange("p (c n) -> p c n", c=C)
        wkT = mem["weights"][:, 0:C * D].rearrange("p (c d) -> p c d", c=C)
        wqT = mem["adjT"][:, 0:C * D].rearrange("p (c d) -> p c d", c=C)
        w_rows = mem["rows_out"][:, 0, :]
        result = mem["rows_out"][:, 1, :]
        h2_tile = mem["h"][:, 0, :]
        x1_tile = mem["h"][:, 1, :]
        h2T = mem["hT"][:, 0:2 * D].bitcast(F32)
        qT = mem["hT"][:, 2 * D:4 * D].bitcast(F32)
        wide = [x1[:].rearrange("p t d -> p (t d)")[:, k * NP:(k + 1) * NP] for k in range(4)]
        bias_of, scale_of, score, factor = wide
        factor_blocks = factor.rearrange("p (b r j) -> p r b j", r=QUADS, j=Q)
        off_diag = mem["bias"][:, 0:P]
        diag = mem["bias"][:, P:2 * P]

        bqT = sb("bqT", [P, C], F32)
        bkT = sb("bkT", [P, C], F32)
        pair_ids = sb("pair_ids", [EROWS, ECOLS, 2], I32)
        places = sb("places", [EROWS, ECOLS], U32)
        place = sb("place", [EROWS, 1], U32)
        held = sb("held_scatter", [P, 1], F32)
        top = sb("top", [P, 1], F32)
        minus_top = sb("minus_top", [P, 1], F32)
        total = sb("total", [P, 1], F32)
        share = sb("share", [P, 1], F32)
        x1_dram = nc.dram_tensor("x1_tiles", [P, T * D], F32).ap()
        listed_dram = nc.dram_tensor("listed_pairs", [N * N, 1], F32).ap()
        listed_rows = listed_dram.rearrange("(r c) a -> r (c a)", c=N)

        ps_T, ps_P, ps_O = (psum[:, b, :] for b in (0, 1, 4))
        ps_S = [psum[:, 2 + k, :] for k in range(2)]

        small_in = sem("small_in")
        x1_saved = sem("x1_saved")
        w_rows_in = sem("w_rows_in")
        wT_done = sem("wT_done")
        wT_kept = sem("wT_kept")
        h2_made = sem("h2_made")
        h2_kept = sem("h2_kept")
        h2T_done = sem("h2T_done")
        h2T_kept = sem("h2T_kept")
        k_done = sem("k_done")
        k_kept = sem("k_kept")
        wide_clear = sem("wide_clear")
        zeros_stored = sem("zeros_stored")
        places_done = sem("places_done")
        place_done = sem("place_done")
        scattered = sem("scattered")
        diag_blank = sem("diag_blank")
        diag_done = sem("diag_done")
        tile_in = sem("tile_in")
        q_tile = sem("q_tile")
        qh_done = sem("qh_done")
        qh_kept = sem("qh_kept")
        q_done = sem("q_done")
        q_kept = sem("q_kept")
        chain = sem("chain")
        dots_done = sem("dots_done")
        dots_used = sem("dots_used")
        top_done = sem("top_done")
        exp_done = sem("exp_done")
        factor_done = sem("factor_done")
        meanT_done = sem("meanT_done")
        meanT_kept = sem("meanT_kept")
        product_done = sem("product_done")
        result_done = sem("result_done")
        result_stored = sem("result_stored")

        def dots(head, k):
            return ps_S[(head * len(COLS) + k) % 2]

        def of_tile(array, t):
            return array.rearrange("p (r c) -> p r c", r=QUADS)[:, :, bass.ds(t * Q, Q)]

        def quads(array):
            return array.rearrange("p (r i) -> p r i", r=QUADS)

        LOADS = 2 * QUADS + 1
        block = ctx.enter_context(nc.Block())

        @block.sync
        def _(sp):
            sp.dma_start(pair_ids[:], pairs.rearrange("(p c) k -> p c k", p=EROWS)).then_inc(small_in, 16)
            for k in range(C):
                sp.dma_start(bqT[:, k:k + 1], bq.rearrange("(c p a) -> c p a", p=P, a=1)[k]).then_inc(small_in, 16)
                sp.dma_start(bkT[:, k:k + 1], bk.rearrange("(c p a) -> c p a", p=P, a=1)[k]).then_inc(small_in, 16)
            sp.dma_start(x1_dram, x1[:].rearrange("p t d -> p (t d)")).then_inc(x1_saved, 16)
            for n in range(2 * C):
                w = wk if n < C else wq
                wait(sp, wT_done, n)
                sp.dma_start(w_rows, w[(n % C) * P:(n % C + 1) * P, :]).then_inc(w_rows_in, 16)

            sp.wait_ge(wide_clear, 1)
            with sp.Fori(0, T - 1) as t:
                sp.dma_start(listed_rows[bass.ds(t * P, P), :], score[:, 0:N]).then_inc(zeros_stored, 16)
            sp.dma_start(listed_rows[(T - 1) * P:N, :], score[0:N - (T - 1) * P, 0:N]).then_inc(zeros_stored, 16)
            sp.wait_ge(zeros_stored, 16 * T)
            sp.wait_ge(scattered, 16 * ECOLS)

            def tile(t, last):
                wait(sp, result_done, t)
                for q, a, b in quad_parts(last, SHORT):
                    at, to = bass.ds(q * QUARTER + t * Q + a, b - a), slice(q * Q + a, q * Q + b)
                    sp.dma_start(bias_of[to, 0:N], adj[at, :]).then_inc(tile_in, 16)
                    sp.dma_start(scale_of[to, 0:N], listed_rows[at, :]).then_inc(tile_in, 16)
                sp.dma_start(x1_tile, x1_dram[:, bass.ds(t * D, D)]).then_inc(tile_in, 16)
                sp.wait_ge(result_done, t + 1)
                for q, a, b in quad_parts(last, SHORT):
                    sp.dma_start(out[bass.ds(q * QUARTER + t * Q + a, b - a), :],
                                 result[q * Q + a:q * Q + b, :]).then_inc(result_stored, 16)

            tile(0, False)
            with sp.Fori(1, T - 1) as t:
                tile(t, False)
            tile(T - 1, True)
            sp.wait_ge(result_stored, 16 * (QUADS * (T - 1) + len(quad_parts(True, SHORT))))

        @block.gpsimd
        def _(pool):
            nc.gpsimd.memset(off_diag, 1.0)
            nc.gpsimd.memset(diag, 0.0).then_inc(diag_blank, 1)
            pool.wait_ge(diag_blank, 1)
            for block_, fill in ((off_diag, 0.0), (diag, SELF_SCORE)):
                ins = nc.gpsimd.affine_select(out=block_, in_=block_, compare_op=ALU.not_equal, fill=fill, base=0,
                                              pattern=[[-1, P]], channel_multiplier=1)
            ins.then_inc(diag_done, 1)

            pool.wait_ge(places_done, 1)
            pool.wait_ge(zeros_stored, 16 * T)

            def scatter(j):
                wait(pool, scattered, j * 16)
                nc.gpsimd.tensor_copy(place[:], places[:, bass.ds(j, 1)]).then_inc(place_done, 1)
                pool.wait_ge(place_done, j + 1)
                nc.gpsimd.tensor_tensor(held[:], ones[:], ones[:], ALU.mult)
                nc.gpsimd.indirect_dma_start(out=listed_dram, in_=ones[0:EROWS, :], in_offset=None,
                                             out_offset=bass.IndirectOffsetOnAxis(ap=place[:], axis=0)
                                             ).then_inc(scattered, 16)

            scatter(0)
            if ECOLS > 1:
                with pool.Fori(1, ECOLS) as j:
                    scatter(j)

        @block.scalar
        def _(act):
            def make_h2(t):
                wait(act, h2T_done, t)
                wait(act, h2_kept, t)
                nc.scalar.activation(h2_tile, x1[:, t, :], ACT.Relu, bias=nmr[:, bass.ds(t, 1)],
                                     scale=rstd[:, bass.ds(t, 1)]).then_inc(h2_made, 1)
                act.wait_ge(h2_made, t + 1)
                nc.scalar.activation(h2[:, t, :], h2_tile, ACT.Copy).then_inc(h2_kept, 1)

            make_h2(0)
            with act.Fori(1, T) as t:
                make_h2(t)

            def tile(t):
                act.wait_ge(qh_done, t)
                nc.scalar.activation(h2_tile, h2[:, t, :], ACT.Copy).then_inc(q_tile, 1)
                for head in range(HEADS):
                    act.wait_ge(top_done, t * HEADS + head + 1)
                    nc.scalar.activation(score[:, :], score[:, :], ACT.Exp, bias=minus_top[:], scale=1.0,
                                         accum_out=total[:]).then_inc(exp_done, 1)

            act.wait_ge(h2T_done, T)
            act.wait_ge(h2_kept, T)
            with act.Fori(0, T) as t:
                tile(t)

        @block.vector
        def _(dve):
            for n in range(2 * C):
                dve.wait_ge(wT_done, n + 1)
                wT, oc = (wkT, n) if n < C else (wqT, n - C)
                nc.vector.tensor_copy(wT[:, :, oc * P:(oc + 1) * P],
                                      ps_T.rearrange("p (c n) -> p c n", c=C)).then_inc(wT_kept, 1)
            dve.wait_ge(small_in, 16 * (1 + 2 * C))
            nc.vector.scalar_tensor_tensor(out=places[:], in0=pair_ids[:, :, 0], scalar=float(N),
                                           in1=pair_ids[:, :, 1], op0=ALU.mult, op1=ALU.add).then_inc(places_done, 1)

            def keep_k(t):
                dve.wait_ge(h2T_done, t + 1)
                wait(dve, k_done, t)
                nc.vector.tensor_copy(h2T, ps_T).then_inc(h2T_kept, 1)
                dve.wait_ge(k_done, t + 1)
                for c in range(C):
                    ins = nc.vector.tensor_scalar(of_tile(kT[:, c, :], t), quads(ps_P[:, c * P:(c + 1) * P]),
                                                  bkT[:, c:c + 1], None, ALU.add)
                ins.then_inc(k_kept, 1)

            keep_k(0)
            with dve.Fori(1, T) as t:
                keep_k(t)
            dve.wait_ge(x1_saved, 16)
            dve.wait_ge(h2_kept, T)
            nc.vector.memset(x1[:], 0.0).then_inc(wide_clear, 1)
            dve.wait_ge(zeros_stored, 16 * T)
            dve.wait_ge(diag_done, 1)

            LINKS = 5 + HEADS * 4

            def tile(t, loads):
                made = [0]

                def link(ins):
                    made[0] += 1
                    ins.then_inc(chain, 1)
                    dve.wait_ge(chain, t * LINKS + made[0])

                dve.wait_ge(qh_done, t + 1)
                wait(dve, q_done, t)
                nc.vector.tensor_copy(h2T, ps_T).then_inc(qh_kept, 1)
                dve.wait_ge(q_done, t + 1)
                wait(dve, dots_done, t * HEADS * len(COLS))
                for c in range(C):
                    ins = nc.vector.tensor_scalar(qT[:, c * P:(c + 1) * P], ps_P[:, c * P:(c + 1) * P],
                                                  bqT[:, c:c + 1], None, ALU.add)
                ins.then_inc(q_kept, 1)

                dve.wait_ge(tile_in, loads)
                link(nc.vector.tensor_scalar(bias_of, bias_of, 1.0, None, ALU.is_equal))
                link(nc.vector.scalar_tensor_tensor(out=scale_of, in0=scale_of, scalar=float(DK) ** -0.5,
                                                    in1=bias_of, op0=ALU.mult, op1=ALU.mult))
                link(nc.vector.tensor_scalar(bias_of, bias_of, -1.0, MASKED, ALU.add, ALU.mult))
                own_scale, own_bias = of_tile(scale_of, t), of_tile(bias_of, t)
                nc.vector.tensor_tensor(own_scale, own_scale, quads(off_diag), ALU.mult)
                link(nc.vector.tensor_tensor(own_bias, own_bias, quads(off_diag), ALU.mult))
                link(nc.vector.tensor_tensor(own_bias, own_bias, quads(diag), ALU.add))

                for head in range(HEADS):
                    for k, (c, n) in enumerate(COLS):
                        dve.wait_ge(dots_done, (t * HEADS + head) * len(COLS) + k + 1)
                        ins = nc.vector.tensor_tensor(score[:, c:c + n], dots(head, k)[:, 0:n], scale_of[:, c:c + n],
                                                      ALU.mult)
                        ins.then_inc(dots_used, 1)
                    dve.wait_ge(dots_used, (t * HEADS + head + 1) * len(COLS))
                    link(nc.vector.tensor_tensor(score, score, bias_of, ALU.add))
                    link(nc.vector.tensor_reduce(top[:], score, AX.X, ALU.max))
                    nc.vector.tensor_scalar(minus_top[:], top[:], -1.0, None, ALU.mult).then_inc(top_done, 1)
                    dve.wait_ge(exp_done, t * HEADS + head + 1)
                    link(nc.vector.reciprocal(share[:], total[:]))
                    link(nc.vector.tensor_scalar(share[:], share[:], 1.0 / HEADS, None, ALU.mult))
                    for r in range(QUADS):
                        prob, mean = score[:, r * QUARTER:(r + 1) * QUARTER], factor_blocks[:, r]
                        prob = prob.rearrange("p (b j) -> p b j", j=Q)
                        if head == 0:
                            ins = nc.vector.tensor_scalar(mean, prob, share[:], None, ALU.mult)
                        else:
                            ins = nc.vector.scalar_tensor_tensor(out=mean, in0=prob, scalar=share[:], in1=mean,
                                                                 op0=ALU.mult, op1=ALU.add)
                    ins.then_inc(factor_done, 1)
                    dve.wait_ge(factor_done, t * HEADS + head + 1)

                for g, (b, n) in enumerate(GROUPS):
                    dve.wait_ge(meanT_done, t * len(GROUPS) + g + 1)
                    nc.vector.tensor_copy(score[:, b * P:(b + n) * P], ps_T[:, 0:n * P]).then_inc(meanT_kept, 1)
                dve.wait_ge(product_done, t + 1)
                wait(dve, result_stored, t * 16 * QUADS)
                nc.vector.tensor_tensor(result, ps_O, x1_tile, ALU.add).then_inc(result_done, 1)

            tile(0, 16 * LOADS)
            with dve.Fori(1, T - 1) as t:
                tile(t, (t + 1) * 16 * LOADS)
            tile(T - 1, 16 * (LOADS * (T - 1) + 2 * len(quad_parts(True, SHORT)) + 1))

        @block.tensor
        def _(pe):
            for n in range(2 * C):
                pe.wait_ge(w_rows_in, 16 * (n + 1))
                wait(pe, wT_kept, n)
                for c in range(C):
                    mm = nc.tensor.transpose(ps_T[:, c * P:(c + 1) * P], w_rows[:, c * P:(c + 1) * P], ident[:])
                mm.then_inc(wT_done, 1)
            pe.wait_ge(wT_kept, 2 * C)

            def transpose_h2(done):
                for c in range(C):
                    mm = nc.tensor.transpose(ps_T[:, c * P:(c + 1) * P], h2_tile[:, c * P:(c + 1) * P], ident[:])
                mm.then_inc(done, 1)

            def project(wT, done):
                for c in range(C):
                    for k in range(C):
                        mm = nc.tensor.matmul(ps_P[:, c * P:(c + 1) * P], wT[:, k, c * P:(c + 1) * P],
                                              h2T[:, k * P:(k + 1) * P], start=(k == 0), stop=(k == C - 1))
                mm.then_inc(done, 1)

            def keys(t):
                pe.wait_ge(h2_made, t + 1)
                wait(pe, h2T_kept, t)
                transpose_h2(h2T_done)
                pe.wait_ge(h2T_kept, t + 1)
                wait(pe, k_kept, t)
                project(wkT, k_done)

            keys(0)
            with pe.Fori(1, T) as t:
                keys(t)
            pe.wait_ge(k_kept, T)
            pe.wait_ge(h2_kept, T)

            def tile(t):
                pe.wait_ge(q_tile, t + 1)
                wait(pe, qh_kept, t)
                transpose_h2(qh_done)
                pe.wait_ge(qh_kept, t + 1)
                wait(pe, q_kept, t)
                project(wqT, q_done)
                pe.wait_ge(q_kept, t + 1)
                for head in range(HEADS):
                    c, lanes = head * DK // P, slice(head * DK % P, head * DK % P + DK)
                    for k, (col, n) in enumerate(COLS):
                        wait(pe, dots_used, (t * HEADS + head) * len(COLS) + k - 1)
                        nc.tensor.matmul(dots(head, k)[:, 0:n], qT[lanes, c * P:(c + 1) * P],
                                         kT[lanes, c, col:col + n], start=True, stop=True).then_inc(dots_done, 1)
                pe.wait_ge(factor_done, (t + 1) * HEADS)
                for g, (b, n) in enumerate(GROUPS):
                    wait(pe, meanT_kept, t * len(GROUPS) + g)
                    for j in range(n):
                        mm = nc.tensor.transpose(ps_T[:, j * P:(j + 1) * P], factor[:, (b + j) * P:(b + j + 1) * P],
                                                 ident[:])
                    mm.then_inc(meanT_done, 1)
                pe.wait_ge(meanT_kept, (t + 1) * len(GROUPS))
                wait(pe, result_done, t)
                for j in range(T):
                    mm = nc.tensor.matmul(ps_O, score[:, j * P:(j + 1) * P], h2[:, j, :], start=(j == 0),
                                          stop=(j == T - 1))
                mm.then_inc(product_done, 1)

            tile(0)
            with pe.Fori(1, T) as t:
                tile(t)


_INS = ['x', 'adj', 'L0_gnn_weight', 'L0_gnn_bias', 'L1_gnn_rel_pair_index', 'L1_gnn_Wq', 'L1_gnn_bq',
        'L1_gnn_Wk', 'L1_gnn_bk']


def kernel(**inputs):
    import numpy as _np
    import concourse.bacc as _bacc
    from concourse import mybir as _mybir
    from concourse.bass_utils import run_bass_kernel_spmd as _run

    nc = _bacc.Bacc("TRN2", target_bir_lowering=False, num_devices=1)
    arrays, args = {}, []
    for name in _INS:
        a = _np.ascontiguousarray(inputs[name])
        arrays[f"in_{name}_dram"] = a
        args.append(nc.dram_tensor(f"in_{name}_dram", a.shape, _mybir.dt.from_np(a.dtype), kind="ExternalInput").ap())
    args.append(nc.dram_tensor("out_0_dram", inputs['x'].shape, _mybir.dt.float32, kind="ExternalOutput").ap())
    gnn_kernel(nc, *args)
    r = _run(nc, [arrays], core_ids=[0])
    return r.results[0]["out_0_dram"]
```
